# Optimizing a Trainium2 kernel written in Bass

```python
import numpy as np
import jax
import jax.numpy as jnp

def _softmax(x, axis=-1):
    return jax.nn.softmax(x, axis=axis)
def _gelu(x):
    return jax.nn.gelu(x, approximate=True)
def _silu(x):
    return jax.nn.silu(x)
def _sigmoid(x):
    return jax.nn.sigmoid(x)
def _layernorm(x, axis=-1, eps=1e-5):
    m = jnp.mean(x, axis=axis, keepdims=True)
    v = jnp.var(x, axis=axis, keepdims=True)
    return (x - m) / jnp.sqrt(v + eps)
def _scatter_add(tgt, idx, src, axis=0):
    return tgt.at[idx].add(src)
def _segment_sum(src, seg, n):
    return jax.ops.segment_sum(src, seg, n)

kernel_name = 'mk_conv_seq_d1_conv_nchw256_448106'

def setup_inputs(seed: int = 0):
    np.random.seed(seed)
    _w = jnp.asarray
    def _rec_inputs():
        import jax
        import jax.numpy as jnp
        _gk = jax.random.key(seed)
        x = -0.0003929 + 0.9999 * jax.random.normal(jax.random.fold_in(_gk, 1), (4, 256, 128, 128), jnp.float32)
        return x
    x = _rec_inputs()
    def _L0_conv_setup():
        import jax, jax.numpy as jnp
        import numpy as np
        EPS = 1e-05

        def bilinear_resize(x, Ho, Wo):
            B, C, H, W = x.shape
            ys = jnp.linspace(0.0, H - 1.0, Ho)
            xs = jnp.linspace(0.0, W - 1.0, Wo)
            y0 = jnp.floor(ys).astype(jnp.int32)
            x0 = jnp.floor(xs).astype(jnp.int32)
            y1 = jnp.minimum(y0 + 1, H - 1)
            x1 = jnp.minimum(x0 + 1, W - 1)
            wy = (ys - y0).astype(x.dtype)[None, None, :, None]
            wx = (xs - x0).astype(x.dtype)[None, None, None, :]
            rows = x[:, :, y0, :] * (1 - wy) + x[:, :, y1, :] * wy
            return rows[:, :, :, x0] * (1 - wx) + rows[:, :, :, x1] * wx

        def conv1x1(x, w, b=None):
            y = jnp.einsum('bchw,oc->bohw', x, w)
            if b is not None:
                y = y + b[None, :, None, None]
            return y

        def bn(x, scale, bias):
            return x * (scale / jnp.sqrt(1.0 + EPS))[None, :, None, None] + bias[None, :, None, None]

        def att(x, q_w, q_b, k_w, k_b, v_w, v_b, gamma):
            B, C, H, W = x.shape
            N = H * W
            q = conv1x1(x, q_w, q_b).reshape(B, -1, N)
            k = conv1x1(x, k_w, k_b).reshape(B, -1, N)
            v = conv1x1(x, v_w, v_b).reshape(B, C, N)
            energy = jnp.einsum('bdi,bdj->bij', q, k)
            attn = jax.nn.softmax(energy, axis=-1)
            out = jnp.einsum('bcj,bij->bci', v, attn).reshape(B, C, H, W)
            return gamma * out + x

        def forward(x, conv1_w, bn1_s, bn1_b, q_w, q_b, k_w, k_b, v_w, v_b, att_gamma, bn2_s, bn2_b, conv2_w, bn3_s, bn3_b):
            B, C, H, W = x.shape
            shortcut = x
            out = bilinear_resize(x, H // 2, W // 2)
            out = jax.nn.relu(bn(conv1x1(out, conv1_w), bn1_s, bn1_b))
            out = att(out, q_w, q_b, k_w, k_b, v_w, v_b, att_gamma)
            out = jax.nn.relu(bn(out, bn2_s, bn2_b))
            out = bn(conv1x1(out, conv2_w), bn3_s, bn3_b)
            out = bilinear_resize(out, H, W)
            return jax.nn.relu(out + shortcut)
        key = jax.random.key(seed)
        ks = jax.random.split(key, 16)
        B, C, H, W = (4, 256, 128, 128)
        d = C // 8
        s = lambda k, shape, sc=0.05: jax.random.normal(k, shape, dtype=jnp.float32) * sc
        return {'x': jax.random.normal(ks[0], (B, C, H, W), dtype=jnp.float32), 'conv1_w': s(ks[1], (C, C)), 'bn1_s': jnp.ones((C,), jnp.float32), 'bn1_b': jnp.zeros((C,), jnp.float32), 'q_w': s(ks[2], (d, C)), 'q_b': jnp.zeros((d,), jnp.float32), 'k_w': s(ks[3], (d, C)), 'k_b': jnp.zeros((d,), jnp.float32), 'v_w': s(ks[4], (C, C)), 'v_b': jnp.zeros((C,), jnp.float32), 'att_gamma': jnp.float32(0.5), 'bn2_s': jnp.ones((C,), jnp.float32), 'bn2_b': jnp.zeros((C,), jnp.float32), 'conv2_w': s(ks[5], (C, C)), 'bn3_s': jnp.ones((C,), jnp.float32), 'bn3_b': jnp.zeros((C,), jnp.float32)}
    _L0_conv_all = _L0_conv_setup()
    _L0_conv_in = {k: v for k, v in _L0_conv_all.items() if k in ('conv1_w', 'bn1_s', 'bn1_b', 'q_w', 'q_b', 'k_w', 'k_b', 'v_w', 'v_b', 'att_gamma', 'bn2_s', 'bn2_b', 'conv2_w', 'bn3_s', 'bn3_b', )}
    del _L0_conv_all

    return {
        "x": x,
        "L0_conv_conv1_w": _L0_conv_in["conv1_w"],
        "L0_conv_bn1_s": _L0_conv_in["bn1_s"],
        "L0_conv_bn1_b": _L0_conv_in["bn1_b"],
        "L0_conv_q_w": _L0_conv_in["q_w"],
        "L0_conv_q_b": _L0_conv_in["q_b"],
        "L0_conv_k_w": _L0_conv_in["k_w"],
        "L0_conv_k_b": _L0_conv_in["k_b"],
        "L0_conv_v_w": _L0_conv_in["v_w"],
        "L0_conv_v_b": _L0_conv_in["v_b"],
        "L0_conv_att_gamma": _L0_conv_in["att_gamma"],
        "L0_conv_bn2_s": _L0_conv_in["bn2_s"],
        "L0_conv_bn2_b": _L0_conv_in["bn2_b"],
        "L0_conv_conv2_w": _L0_conv_in["conv2_w"],
        "L0_conv_bn3_s": _L0_conv_in["bn3_s"],
        "L0_conv_bn3_b": _L0_conv_in["bn3_b"],
    }

def reference(x, L0_conv_conv1_w, L0_conv_bn1_s, L0_conv_bn1_b, L0_conv_q_w, L0_conv_q_b, L0_conv_k_w, L0_conv_k_b, L0_conv_v_w, L0_conv_v_b, L0_conv_att_gamma, L0_conv_bn2_s, L0_conv_bn2_b, L0_conv_conv2_w, L0_conv_bn3_s, L0_conv_bn3_b):
    import jax
    import jax.numpy as jnp
    def _L0_conv_ref(x, conv1_w, bn1_s, bn1_b, q_w, q_b, k_w, k_b, v_w, v_b, att_gamma, bn2_s, bn2_b, conv2_w, bn3_s, bn3_b):
        import jax, jax.numpy as jnp
        import numpy as np
        EPS = 1e-05

        def bilinear_resize(x, Ho, Wo):
            B, C, H, W = x.shape
            ys = jnp.linspace(0.0, H - 1.0, Ho)
            xs = jnp.linspace(0.0, W - 1.0, Wo)
            y0 = jnp.floor(ys).astype(jnp.int32)
            x0 = jnp.floor(xs).astype(jnp.int32)
            y1 = jnp.minimum(y0 + 1, H - 1)
            x1 = jnp.minimum(x0 + 1, W - 1)
            wy = (ys - y0).astype(x.dtype)[None, None, :, None]
            wx = (xs - x0).astype(x.dtype)[None, None, None, :]
            rows = x[:, :, y0, :] * (1 - wy) + x[:, :, y1, :] * wy
            return rows[:, :, :, x0] * (1 - wx) + rows[:, :, :, x1] * wx

        def conv1x1(x, w, b=None):
            y = jnp.einsum('bchw,oc->bohw', x, w)
            if b is not None:
                y = y + b[None, :, None, None]
            return y

        def bn(x, scale, bias):
            return x * (scale / jnp.sqrt(1.0 + EPS))[None, :, None, None] + bias[None, :, None, None]

        def att(x, q_w, q_b, k_w, k_b, v_w, v_b, gamma):
            B, C, H, W = x.shape
            N = H * W
            q = conv1x1(x, q_w, q_b).reshape(B, -1, N)
            k = conv1x1(x, k_w, k_b).reshape(B, -1, N)
            v = conv1x1(x, v_w, v_b).reshape(B, C, N)
            energy = jnp.einsum('bdi,bdj->bij', q, k)
            attn = jax.nn.softmax(energy, axis=-1)
            out = jnp.einsum('bcj,bij->bci', v, attn).reshape(B, C, H, W)
            return gamma * out + x

        def forward(x, conv1_w, bn1_s, bn1_b, q_w, q_b, k_w, k_b, v_w, v_b, att_gamma, bn2_s, bn2_b, conv2_w, bn3_s, bn3_b):
            B, C, H, W = x.shape
            shortcut = x
            out = bilinear_resize(x, H // 2, W // 2)
            out = jax.nn.relu(bn(conv1x1(out, conv1_w), bn1_s, bn1_b))
            out = att(out, q_w, q_b, k_w, k_b, v_w, v_b, att_gamma)
            out = jax.nn.relu(bn(out, bn2_s, bn2_b))
            out = bn(conv1x1(out, conv2_w), bn3_s, bn3_b)
            out = bilinear_resize(out, H, W)
            return jax.nn.relu(out + shortcut)
        return forward(x, conv1_w, bn1_s, bn1_b, q_w, q_b, k_w, k_b, v_w, v_b, att_gamma, bn2_s, bn2_b, conv2_w, bn3_s, bn3_b)

    def _gn(v, G=32, eps=1e-5):
        B_, C_, H_, W_ = v.shape
        g = v.reshape(B_, G, C_ // G, H_, W_)
        m = jnp.mean(g, axis=(2, 3, 4), keepdims=True)
        s = jnp.var(g, axis=(2, 3, 4), keepdims=True)
        return ((g - m) / jnp.sqrt(s + eps)).reshape(v.shape)

    def _ln_c(v, eps=1e-6):
        m = jnp.mean(v, axis=1, keepdims=True)
        s = jnp.var(v, axis=1, keepdims=True)
        return (v - m) / jnp.sqrt(s + eps)

    def _ln_t(v, eps=1e-5):
        m = jnp.mean(v, axis=-1, keepdims=True)
        s = jnp.var(v, axis=-1, keepdims=True)
        return (v - m) / jnp.sqrt(s + eps)

    def _to_tokens(v):
        B_, C_, H_, W_ = v.shape
        return v.reshape(B_, C_, H_ * W_).transpose(0, 2, 1)
    def _from_tokens(t, like):
        B_, C_, H_, W_ = like.shape
        return t.transpose(0, 2, 1).reshape(B_, C_, H_, W_)

    x = _L0_conv_ref(x, L0_conv_conv1_w, L0_conv_bn1_s, L0_conv_bn1_b, L0_conv_q_w, L0_conv_q_b, L0_conv_k_w, L0_conv_k_b, L0_conv_v_w, L0_conv_v_b, L0_conv_att_gamma, L0_conv_bn2_s, L0_conv_bn2_b, L0_conv_conv2_w, L0_conv_bn3_s, L0_conv_bn3_b)
    return x


_drawn_inputs = setup_inputs


def setup_inputs(seed=0):
    import zlib

    import numpy as np

    out = dict(_drawn_inputs(seed))
    spreads = {'L0_conv_bn1_s': (1.0, 0.2),
     'L0_conv_bn1_b': (0.0, 0.1),
     'L0_conv_q_b': (0.0, 0.8),
     'L0_conv_k_b': (0.0, 0.8),
     'L0_conv_v_b': (0.0, 0.1),
     'L0_conv_bn2_s': (1.0, 0.2),
     'L0_conv_bn2_b': (0.0, 0.1),
     'L0_conv_bn3_s': (1.0, 0.2),
     'L0_conv_bn3_b': (0.0, 0.1)}
    factors = {'L0_conv_q_w': 8.0, 'L0_conv_k_w': 8.0}
    for name, (base, spread) in spreads.items():
        noise = np.random.default_rng([zlib.crc32(name.encode()), seed]).standard_normal(out[name].shape)
        drawn = base * np.exp(spread * noise) if base else spread * noise
        out[name] = jnp.asarray(drawn.astype(out[name].dtype))
    for name, factor in factors.items():
        out[name] = (out[name] * factor).astype(out[name].dtype)
    return out
```

```python
import concourse.bass as bass
from concourse import mybir
from contextlib import ExitStack

F32 = mybir.dt.float32
F32R = mybir.dt.float32r
F16 = mybir.dt.float16
ACT = mybir.ActivationFunctionType
ALU = mybir.AluOpType
AX = mybir.AxisListType

B, C, H, D = 4, 256, 128, 32
S = H // 2
N = S * S
P = 128
CH = C // P
IB = 512
NB = N // IB
IT = IB // P
JT = N // P
JC = N // IB
EU = IT * JC
BR = IB // S
UR = 8
DR = 8
PIECES = 4
VB = 2
VU = JT // VB
VS = 4
LOG_P = 8.0
V_TOP = 2.0 ** 14
BN = 1.0 / (1.0 + 1e-5) ** 0.5
DN, UP = 6, 5
FIRST_POOL = 1


def attention_block_kernel(nc, x, w1, s1, b1, wq, bq, wk, bk, wv, bv, gamma, s2, b2, w2, s3, b3,
                           ident_d, down_w, up_w, out):
    with ExitStack() as ctx:
        def sb(name, shape, dt=F32):
            return ctx.enter_context(nc.sbuf_tensor(name, shape, dt))

        def bank(name):
            return ctx.enter_context(nc.psum_tensor(name, [P, 512], F32))

        def sem(name):
            return ctx.enter_context(nc.semaphore(name))

        xv = sb("xv", [P, CH * N])
        xr = xv[:, :].rearrange("p (h r c) -> p h r c", h=CH, c=S)
        xr_flat = xv[:, :].rearrange("p (h n) -> p h n", h=CH)
        v32 = xv[:, :].rearrange("p (j c) -> p j c", c=C)
        a = sb("a", [P, CH, N])
        ks = sb("ks", [P, N], F32R)
        qs = sb("qs", [P, N], F32R)
        qm = sb("qm", [3 * D, IB], F32R)
        vh = sb("vh", [P, JT, C + 2], F16)
        vl = sb("vl", [P, JT, C], F16)
        ph = sb("ph", [P, 4, IB], F16)
        pl = sb("pl", [P, 4, IB], F16)
        osb = sb("osb", [P, IT, C])
        hbuf = sb("hbuf", [P, CH, IB])
        win = sb("win", [P, 2, CH, BR + 2, S])
        xres = sb("xres", [P, 4, UR, H])
        xin = sb("xin", [P, 2, DR, H])
        rd = sb("rd", [P, UR // 2 + 1, S])
        rt = sb("rt", [P, UR // 2, 2, S])
        y2 = sb("y2", [P, UR, S])
        cd = sb("cd", [P, UR, S + 1])
        ct = sb("ct", [P, UR, S, 2])
        dd = sb("dd", [P, DR // 2, S])
        dd0 = sb("dd0", [P, DR // 2, S])
        w1t = sb("w1t", [P, CH, C])
        wvt = sb("wvt", [P, CH, C])
        w2t = sb("w2t", [P, CH, C])
        wqk = sb("wqk", [P, CH, 4 * D])
        ident = sb("ident", [P, P])
        dw = sb("dw", [P, S])
        uw = sb("uw", [P, S, 2])
        par = sb("par", [P, 8, CH])
        S1, B1, S2, B2, S3, B3, BV = range(7)
        gam = sb("gam", [P, 1])
        qkb = sb("qkb", [P, 1])
        mx = sb("mx", [P, IT, JC])
        m4 = sb("m4", [P, IT])
        mn = sb("mn", [P, IT])
        mhl = sb("mhl", [P, IT, 2], F32R)
        vmx = sb("vmx", [P, VU])
        vm1 = sb("vm1", [P, 1])
        vma = sb("vma", [1, 1])
        ones = sb("ones", [1, P])
        vg = sb("vg", [P, 4])
        rl = sb("rl", [P, IT])

        acc = [bank(f"acc{i}") for i in range(IT)]
        et = [bank(f"et{i}") for i in range(2)]
        emx = bank("emx")
        wrk = bank("wrk")

        par_ld, wts_ld = sem("par_ld"), sem("wts_ld")
        par_ok, wt_rdy, wt_ok, mem_ok, memv_ok = (sem(n) for n in ("par_ok", "wt_rdy", "wt_ok", "mem_ok", "memv_ok"))
        xin_ld = [sem(f"xin_ld{i}") for i in range(2)]
        xres_ld = [sem(f"xres_ld{i}") for i in range(4)]
        stored = [sem(f"stored{i}") for i in range(4)]
        down_p, down_v = sem("down_p"), sem("down_v")
        up_p, up_v = sem("up_p"), sem("up_v")
        up_added, up_relu = sem("up_added"), sem("up_relu")
        c1_rdy, c1_done = sem("c1_rdy"), sem("c1_done")
        qk_rdy, qk_hi, qk_done = sem("qk_rdy"), sem("qk_hi"), sem("qk_done")
        v_rdy, v_done, vmax_part, vmax_1 = (sem(n) for n in ("v_rdy", "v_done", "vmax_part", "vmax_1"))
        vmax_row, vmax_one, vmax_all = sem("vmax_row"), sem("vmax_one"), sem("vmax_all")
        vscale, vh_rdy, vl_rdy = sem("vscale"), sem("vh_rdy"), sem("vl_rdy")
        qm_rdy, emx_rdy, emx_free, m_link, mt_rdy, m_rdy = (
            sem(n) for n in ("qm_rdy", "emx_rdy", "emx_free", "m_link", "mt_rdy", "m_rdy"))
        et_rdy, p_rdy, pl_rdy, pv_done = sem("et_rdy"), sem("p_rdy"), sem("pl_rdy"), sem("pv_done")
        acc_rdy, rl_rdy, acc_free = sem("acc_rdy"), sem("rl_rdy"), sem("acc_free")
        ot_rdy, ot_done, h_rdy = sem("ot_rdy"), sem("ot_done"), sem("h_rdy")
        cv_rdy, y_rdy = sem("cv_rdy"), sem("y_rdy")

        def at_least(eng, s, value):
            if isinstance(value, int) and value <= 0:
                return
            eng.wait_ge(s, value)

        def walk(eng, enter, block, leave, last_apart=False):
            def batch(b):
                enter(b)
                for n in range(3):
                    block(b, n, n)
                with eng.Fori(0, (NB - 4) // 2) as i:
                    block(b, i * 2 + 3, 3)
                    block(b, i * 2 + 4, 4)
                block(b, NB - 1, NB - 1)
                leave(b)

            batch(0)
            if last_apart:
                with eng.Fori(1, B - 1) as b:
                    batch(b)
                batch(B - 1)
            else:
                with eng.Fori(1, B) as b:
                    batch(b)

        def held(eng, value):
            return value if isinstance(value, int) else eng.snap(value)

        def up_pieces(b, n, c):
            for j in range(PIECES):
                back = 3 if j < 3 else 2
                g = b * NB + n
                if isinstance(g, int) and g < back:
                    continue
                wrap = c < back
                yield (j, g * PIECES - 11 + j, b - 1 if wrap else b, n + NB - back if wrap else n - back,
                       (c - back) % 2, (1 + j) % PIECES)

        LAST_PIECES = range(PIECES * (NB * B - 1) - 11 + PIECES, PIECES * NB * B)

        def late_pieces():
            for u in LAST_PIECES:
                chunk = u // PIECES
                yield (u + 3) % 4, u, B - 1, chunk - (B - 1) * NB, chunk % 2, u % PIECES

        def xslot(j):
            return (j + 1) % 4

        def piece_rows(n, k):
            return k % 2, (n * (2 * BR) + (k // 2) * UR)

        def dram_rows(t, b, half, row, rows):
            v = t[bass.ds(b, 1), half * P:(half + 1) * P, bass.ds(row, rows), :]
            return v.rearrange("o p r c -> (o p) r c")

        V_PIECES = PIECES - FIRST_POOL
        XRES_FIRST = NB * V_PIECES // 4
        POOL_FIRST = DN * NB * FIRST_POOL

        def down_count(b, d):
            return (b - 1) * (DN * NB * PIECES) + (POOL_FIRST + DN * d)

        nc.disable_value_cache = True
        block = ctx.enter_context(nc.Block())

        @block.sync
        def _(sp):
            npar = 0
            for i, t in ((S1, s1), (B1, b1), (S2, s2), (B2, b2), (S3, s3), (B3, b3), (BV, bv)):
                sp.dma_start(par[:, i, :], t.rearrange("(h p) -> p h", p=P), allow_slow_non_contiguous=True).then_inc(par_ld, 16)
                npar += 1
            for i, t in enumerate((bk, bk, bq, bq)):
                sp.dma_start(qkb[i * D:(i + 1) * D, :], t.unsqueeze(1)).then_inc(par_ld, 16)
                npar += 1
            sp.dma_start(gam[:], gamma.partition_broadcast(P)).then_inc(par_ld, 16)
            sp.dma_start(dw[:], down_w.partition_broadcast(P)).then_inc(par_ld, 16)
            sp.dma_start(uw[:], up_w.partition_broadcast(P)).then_inc(par_ld, 16)
            assert npar + 3 == N_PAR

            for d in range(NB * PIECES):
                ck, j = divmod(d, PIECES)
                if d == 2:
                    sp.dma_start(ident[:], ident_d).then_inc(wts_ld, 16)
                    for dst, t in ((osb[:, 0:2, :], w1), (osb[:, 2:4, :], wv), (hbuf[:, :, 0:C], w2)):
                        sp.dma_start(dst, t.rearrange("(o p) c -> p o c", p=P)).then_inc(wts_ld, 16)
                    sp.dma_start(hbuf[0:D, 0, C:2 * C], wk).then_inc(wts_ld, 16)
                    sp.dma_start(hbuf[0:D, 1, C:2 * C], wq).then_inc(wts_ld, 16)
                src = dram_rows(x, 0, j % 2, (2 * ck + j // 2) * DR, DR)
                if j < V_PIECES:
                    i = ck * V_PIECES + j
                    at_least(sp, down_v, DN * (i - 3))
                    sp.dma_start(xres[:, i % 4], src).then_inc(xres_ld[i % 4], 16)
                else:
                    i = ck * FIRST_POOL + j - V_PIECES
                    at_least(sp, down_p, DN * (i - 1))
                    sp.dma_start(xin[:, i % 2], src).then_inc(xin_ld[i % 2], 16)

            def load_shortcut(j, u, b, n, k):
                half, row = piece_rows(n, k)
                s = xslot(j)
                uses = (u - s) // 4 if isinstance(u, int) else None
                at_least(sp, stored[s], (u - s) * 4 if uses is None else uses * 16)
                if isinstance(u, int) and u < 4:
                    sp.wait_ge(down_v, DN * NB * V_PIECES)
                sp.dma_start(xres[:, s], dram_rows(x, b, half, row, UR)).then_inc(xres_ld[s], 16)

            def store(j, u, b, n, k):
                half, row = piece_rows(n, k)
                sp.wait_ge(up_relu, u + 1)
                sp.dma_start(dram_rows(out, b, half, row, UR), xres[:, xslot(j)]).then_inc(stored[xslot(j)], 16)

            def enter(b):
                pass

            def blk(b, n, c):
                ups = {j: (u, ub, un, k) for j, u, ub, un, _, k in up_pieces(b, n, c)}
                for j in range(PIECES):
                    if j in ups:
                        load_shortcut(j, *ups[j])
                    if not (isinstance(b, int) and b == B - 1):
                        i = n * PIECES + j
                        sp.wait_ge(down_p, down_count(b + 1, i - 1))
                        sp.dma_start(xin[:, j % 2], dram_rows(x, b + 1, j % 2, (n * 2 + j // 2) * DR, DR)).then_inc(
                            xin_ld[j % 2], 16)
                    if j in ups:
                        store(j, *ups[j])

            def leave(b):
                pass

            walk(sp, enter, blk, leave, last_apart=True)
            for j, u, ub, un, _, k in late_pieces():
                load_shortcut(j, u, ub, un, k)
                if u - 1 in LAST_PIECES:
                    jj, uu, bb, nn, _, kk = last
                    store(jj, uu, bb, nn, kk)
                last = (j, u, ub, un, _, k)
            jj, uu, bb, nn, _, kk = last
            store(jj, uu, bb, nn, kk)
            for s in range(4):
                sp.wait_ge(stored[s], 16 * B * NB)

        def down_piece(eng, ops, s, count, src, tmp, dst, first_small_row):
            pair = src.rearrange("p (r two) c -> p r two c", two=2)
            even, odd = pair[:, :, 0, :], pair[:, :, 1, :]
            rw = dw[:, bass.ds(first_small_row, DR // 2)].unsqueeze(2).broadcast_to([P, DR // 2, H])
            cw = dw[:, :].unsqueeze(1).broadcast_to([P, DR // 2, S])
            cols = even.rearrange("p r (c two) -> p r c two", two=2)
            ops.tensor_tensor(odd, odd, even, ALU.subtract).then_inc(s, 1)
            eng.wait_ge(s, count + 1)
            ops.tensor_tensor(odd, odd, rw, ALU.mult).then_inc(s, 1)
            eng.wait_ge(s, count + 2)
            ops.tensor_tensor(even, even, odd, ALU.add).then_inc(s, 1)
            eng.wait_ge(s, count + 3)
            ops.tensor_tensor(tmp, cols[:, :, :, 1], cols[:, :, :, 0], ALU.subtract).then_inc(s, 1)
            eng.wait_ge(s, count + 4)
            ops.tensor_tensor(tmp, tmp, cw, ALU.mult).then_inc(s, 1)
            eng.wait_ge(s, count + 5)
            ops.tensor_tensor(dst, cols[:, :, :, 0], tmp, ALU.add).then_inc(s, 1)

        @block.gpsimd
        def _(pool):
            ops = nc.gpsimd
            ops.memset(ks[3 * D:P, :].bitcast(F32), 1.0).then_inc(mem_ok, 1)
            pool.wait_ge(mem_ok, 1)
            ops.memset(vh[:, :, C:C + 2], 1.0).then_inc(mem_ok, 1)
            pool.wait_ge(mem_ok, 2)
            ops.memset(ones[:], 1.0).then_inc(mem_ok, 1)
            pool.wait_ge(mem_ok, 3)
            ops.memset(cd[:], 0.0).then_inc(mem_ok, 1)
            pool.wait_ge(mem_ok, 4)
            pool.wait_ge(par_ld, 16 * N_PAR)
            for i in range(NB * FIRST_POOL):
                ck, j = divmod(i, FIRST_POOL)
                j += V_PIECES
                pool.wait_ge(xin_ld[i % 2], 16 * (i // 2 + 1))
                small = (2 * ck + j // 2) * (DR // 2)
                down_piece(pool, ops, down_p, DN * i, xin[:, i % 2], dd[:], xr[:, j % 2, bass.ds(small, DR // 2), :], small)

            def up_piece(u, n, par_, k):
                half, q = k % 2, k // 2
                w = win[:, par_, half, q * (BR // 2):q * (BR // 2) + BR // 2 + 2, :]
                R = UR // 2
                base = u * UP
                ops.tensor_tensor(rd[:], w[:, 1:R + 2, :], w[:, 0:R + 1, :], ALU.subtract).then_inc(up_p, 1)
                pool.wait_ge(up_p, base + 1)
                first = n * BR + q * R
                for parity in range(2):
                    wt = uw[:, bass.ds(first, R), parity:parity + 1].broadcast_to([P, R, S])
                    last = ops.tensor_tensor(rt[:, :, parity, :], rd[:, parity:parity + R, :], wt, ALU.mult)
                last.then_inc(up_p, 1)
                pool.wait_ge(up_p, base + 2)
                at_least(pool, up_added, u)
                mid = w[:, 1:R + 1, :].unsqueeze(2).broadcast_to([P, R, 2, S])
                ops.tensor_tensor(y2[:].rearrange("p (r two) c -> p r two c", two=2), mid, rt[:], ALU.add).then_inc(up_p, 1)
                pool.wait_ge(up_p, base + 3)
                ops.tensor_tensor(cd[:, :, 1:S], y2[:, :, 1:S], y2[:, :, 0:S - 1], ALU.subtract).then_inc(up_p, 1)
                pool.wait_ge(up_p, base + 4)
                for parity in range(2):
                    wt = uw[:, :, parity].unsqueeze(1).broadcast_to([P, UR, S])
                    last = ops.tensor_tensor(ct[:, :, :, parity], cd[:, :, parity:parity + S], wt, ALU.mult)
                last.then_inc(up_p, 1)

            def enter(b):
                pass

            def blk(b, n, c):
                ups = {j: (u, un, pr, k) for j, u, _, un, pr, k in up_pieces(b, n, c)}
                g = b * NB + n
                for j in range(PIECES):
                    if j in ups:
                        if j == 3:
                            pool.wait_ge(y_rdy, g * 2)
                        up_piece(*ups[j])
                    if not (isinstance(b, int) and b == B - 1):
                        if c == 0 and j == 0:
                            pool.wait_ge(vl_rdy, (b + 1) * VS)
                        i = n * PIECES + j
                        fills = NB * FIRST_POOL // 2
                        pool.wait_ge(xin_ld[j % 2], b * (16 * NB * PIECES // 2) + n * 32 + (16 * (fills + j // 2 + 1)))
                        small = (n * 2 + j // 2) * (DR // 2)
                        down_piece(pool, ops, down_p, down_count(b + 1, i), xin[:, j % 2], dd[:],
                                   xr[:, j % 2, bass.ds(small, DR // 2), :], small)

            def leave(b):
                pass

            walk(pool, enter, blk, leave, last_apart=True)
            for j, u, ub, un, pr, k in late_pieces():
                if k == 0 and un == NB - 2:
                    pool.wait_ge(y_rdy, 2 * NB * B)
                up_piece(u, un, pr, k)

        @block.scalar
        def _(act):
            ops = nc.scalar

            def weights_of(s, t):
                act.wait_ge(et_rdy, s + 1)
                at_least(act, pv_done, s - 3)
                ops.activation(ph[:, t % 4, :], et[t % 2][:, :], ACT.Exp)
                ops.activation(et[t % 2][:, :], et[t % 2][:, :], ACT.Exp).then_inc(p_rdy, 1)

            def relu_h(chunk, half):
                act.wait_ge(ot_done, chunk * 2 + (half + 1))
                ops.activation(hbuf[:, half, :], hbuf[:, half, :], ACT.Relu, bias=par[:, B2, half:half + 1],
                               scale=par[:, S2, half:half + 1]).then_inc(h_rdy, 1)

            def bn3(chunk, par_, half, first, last):
                act.wait_ge(cv_rdy, chunk * 2 + (half + 1))
                if half == 0:
                    at_least(act, up_p, (chunk - 1) * (UP * PIECES))
                    at_least(act, y_rdy, chunk * 2)
                new, old = win[:, par_, half], win[:, 1 - par_, half]
                cv = wrk[:, :].rearrange("p (r c) -> p r c", c=S)
                jobs = [(new[:, 0:1, :], cv[:, 0:1, :])] if first else [(old[:, BR + 1:BR + 2, :], cv[:, 0:1, :])]
                if last:
                    jobs.append((new[:, BR + 1:BR + 2, :], cv[:, BR - 1:BR, :]))
                if not first:
                    ops.copy(new[:, 0, :], old[:, BR, :])
                for dst, src in jobs + [(new[:, 1:BR + 1, :], cv)]:
                    done = ops.activation(dst, src, ACT.Identity, bias=par[:, B3, half:half + 1], scale=par[:, S3, half:half + 1])
                done.then_inc(y_rdy, 1)

            def final_relu(j, u):
                act.wait_ge(up_added, u + 1)
                ops.activation(xres[:, xslot(j)], xres[:, xslot(j)], ACT.Relu).then_inc(up_relu, 1)

            act.wait_ge(par_ok, PAR_OPS)

            def enter(b):
                at_least(act, ot_done, b * (2 * NB))
                for u in range(2 * NB):
                    ck, oh = divmod(u, 2)
                    act.wait_ge(c1_rdy, b * (2 * NB) + (u + 1))
                    ops.activation(a[:, oh, ck * IB:(ck + 1) * IB], acc[u % 4][:, :], ACT.Relu, bias=par[:, B1, oh:oh + 1],
                                   scale=par[:, S1, oh:oh + 1]).then_inc(c1_done, 1)
                for ck in range(NB):
                    cs = slice(ck * IB, (ck + 1) * IB)
                    act.wait_ge(qk_rdy, b * NB + (ck + 1))
                    ps = acc[ck % 4]
                    ops.activation(ks[0:2 * D, cs], ps[0:2 * D, :], ACT.Identity, bias=qkb[0:2 * D, :])
                    ops.activation(qs[0:2 * D, cs], ps[2 * D:4 * D, :], ACT.Identity, bias=qkb[2 * D:4 * D, :])
                    ops.activation(qs[2 * D:3 * D, cs], ps[2 * D:3 * D, :], ACT.Identity,
                                   bias=qkb[2 * D:3 * D, :]).then_inc(qk_hi, 1)
                for v in range(VU):
                    act.wait_ge(v_rdy, b * VU + (v + 1))
                    ops.activation(v32[:, v * VB:(v + 1) * VB, :], acc[v % 4][:, :].rearrange("p (j c) -> p j c", c=C),
                                   ACT.Copy).then_inc(v_done, 1)
                weights_of(b * (NB * JT), 0)
                weights_of(b * (NB * JT) + 1, 1)
                act.wait_ge(vscale, b * 4 + 4)
                for q in range(VS):
                    js = slice(q * (JT // VS), (q + 1) * (JT // VS))
                    ops.activation(vh[:, js, 0:C], v32[:, js, :], ACT.Copy, scale=vg[:, 2:3]).then_inc(vh_rdy, 1)

            def blk(b, n, c):
                g = b * NB + n
                s0 = g * JT
                ups = {j: u for j, u, _, _, _, _ in up_pieces(b, n, c)}
                for t in range(JT):
                    if c > 0 and t in (T_OT[0] + 2, T_OT[1] + 2):
                        relu_h(g - 1, T_OT.index(t - 2))
                    if t in (T_CV[0] + 1, T_CV[1] + 1) and not (isinstance(g, int) and g == 0):
                        bn3(g - 1, (c - 1) % 2, T_CV.index(t - 1), c == 1, c == 0)
                    if t in T_RELU and T_RELU.index(t) in ups:
                        j = T_RELU.index(t)
                        final_relu(j, ups[j])
                    if t + 2 < JT or c < NB - 1:
                        weights_of(s0 + (t + 2), (t + 2) % JT)

            def leave(b):
                g1 = b * NB + NB
                for half in range(2):
                    relu_h(g1 - 1, half)

            walk(act, enter, blk, leave)
            late = list(late_pieces())
            for j, u, _, un, _, k in late:
                if k == 0 and un == NB - 2:
                    for half in range(2):
                        bn3(NB * B - 1, (NB - 1) % 2, half, False, True)
                final_relu(j, u)

        @block.vector
        def _(dve):
            ops = nc.vector
            ops.memset(qs[3 * D:P, :].bitcast(F32), 0.0).then_inc(memv_ok, 1)
            dve.wait_ge(par_ld, 16 * N_PAR)
            for i in (S1, S2, S3):
                ops.tensor_scalar(par[:, i, :], par[:, i, :], BN, None, ALU.mult)
            ops.tensor_scalar(par[:, BV, :], par[:, BV, :], gam[:, 0:1], None, ALU.mult).then_inc(par_ok, 1)
            dve.wait_ge(par_ok, 1)
            ops.tensor_tensor(par[:, BV, :], par[:, BV, :], par[:, S2, :], ALU.mult).then_inc(par_ok, 1)
            dve.wait_ge(par_ok, 2)
            ops.tensor_tensor(par[:, B2, :], par[:, B2, :], par[:, BV, :], ALU.add).then_inc(par_ok, 1)

            def transposed_weights():
                for i, dst in enumerate((w1t, wvt, w2t)):
                    dve.wait_ge(wt_rdy, i + 1)
                    ops.tensor_copy(dst[:].rearrange("p h c -> p (h c)"), acc[i][:, :])
                dve.wait_ge(wt_rdy, 4)
                for i in range(4):
                    last = ops.tensor_copy(wqk[:, :, i * D:(i + 1) * D],
                                           acc[3][:, 0:4 * D].rearrange("p (w h d) -> p w h d", w=2, h=CH)[:, i // 2])
                last.then_inc(wt_ok, 1)

            for i in range(NB * V_PIECES):
                ck, j = divmod(i, V_PIECES)
                if i == 2:
                    transposed_weights()
                dve.wait_ge(xres_ld[i % 4], 16 * (i // 4 + 1))
                small = (2 * ck + j // 2) * (DR // 2)
                down_piece(dve, ops, down_v, DN * i, xres[:, i % 4], dd0[:], xr[:, j % 2, bass.ds(small, DR // 2), :], small)

            def row_max(g, u):
                dve.wait_ge(emx_rdy, g * EU + (u + 1))
                ops.reduce_max(mx[:, u // JC, u % JC:u % JC + 1], emx[:, :], AX.X).then_inc(emx_free, 1)

            def shift(g):
                dve.wait_ge(emx_free, g * EU + EU)
                ops.reduce_max(m4[:], mx[:], AX.X).then_inc(m_link, 1)
                dve.wait_ge(m_link, g * 4 + 1)
                ops.tensor_scalar(mn[:], m4[:], -1.0, LOG_P, ALU.mult, ALU.add).then_inc(m_link, 1)
                dve.wait_ge(m_link, g * 4 + 2)
                ops.tensor_copy(mhl[:, :, 0], mn[:]).then_inc(m_link, 1)
                dve.wait_ge(m_link, g * 4 + 3)
                ops.tensor_tensor(mhl[:, :, 1], mn[:], mhl[:, :, 0].bitcast(F32), ALU.subtract).then_inc(m_link, 1)

            def shift_rows(g, n):
                dve.wait_ge(mt_rdy, g + 1)
                ops.tensor_copy(qs[3 * D:3 * D + 2, bass.ds(n * IB, IB)], wrk[0:2, :]).then_inc(m_rdy, 1)

            def low_parts(s, t):
                dve.wait_ge(p_rdy, s + 1)
                at_least(dve, pv_done, s - 3)
                ops.tensor_tensor(pl[:, t % 4, :], et[t % 2][:, :], ph[:, t % 4, :], ALU.subtract).then_inc(pl_rdy, 1)

            def copy_queries(n):
                ops.tensor_copy(qm[:, :], qs[0:3 * D, bass.ds(n * IB, IB)].bitcast(F32)).then_inc(qm_rdy, 1)

            def residual(chunk, n, half):
                dve.wait_ge(ot_rdy, chunk * 2 + (half + 1))
                at_least(dve, cv_rdy, chunk * 2)
                ops.tensor_tensor(hbuf[:, half, :], wrk[:, :], a[:, half, bass.ds(n * IB, IB)], ALU.add).then_inc(ot_done, 1)

            def add_piece(j, u):
                dve.wait_ge(up_p, u * UP + UP)
                dve.wait_ge(xres_ld[xslot(j)], (u - xslot(j)) * 4 + 16 * (XRES_FIRST + 1))
                xs = xres[:, xslot(j)]
                ops.tensor_tensor(xs, xs, ct[:].rearrange("p r c two -> p r (c two)"), ALU.add).then_inc(up_v, 1)
                dve.wait_ge(up_v, u + 1)
                xs4 = xs.rearrange("p r (c two) -> p r c two", two=2)
                ops.tensor_tensor(xs4, xs4, y2[:].unsqueeze(3).broadcast_to([P, UR, S, 2]), ALU.add).then_inc(up_added, 1)

            def enter(b):
                for ck in range(NB):
                    cs = slice(ck * IB, (ck + 1) * IB)
                    dve.wait_ge(qk_hi, b * NB + (ck + 1))
                    ps = acc[ck % 4]
                    ops.tensor_copy(ks[2 * D:3 * D, cs], ks[0:D, cs].bitcast(F32))
                    for t, r in ((ks, slice(D, 2 * D)), (qs, slice(2 * D, 3 * D))):
                        last = ops.scalar_tensor_tensor(t[r, cs], ps[r, :], qkb[r, :], t[r, cs].bitcast(F32), ALU.add, ALU.subtract)
                    last.then_inc(qk_done, 1)
                dve.wait_ge(qk_done, b * NB + 1)
                copy_queries(0)
                for v in range(VU):
                    for u in (2 * v, 2 * v + 1):
                        row_max(b * NB, u)
                    dve.wait_ge(v_done, b * VU + (v + 1))
                    ops.tensor_reduce(vmx[:, v:v + 1], v32[:, v * VB:(v + 1) * VB, :], AX.XY, ALU.max,
                                      apply_absolute_value=True).then_inc(vmax_part, 1)
                shift(b * NB)
                dve.wait_ge(vmax_part, b * VU + VU)
                ops.reduce_max(vm1[:], vmx[:], AX.X).then_inc(vmax_1, 1)
                shift_rows(b * NB, 0)
                dve.wait_ge(vmax_row, b + 1)
                ops.reduce_max(vma[:], emx[0:1, 0:P], AX.X).then_inc(vmax_one, 1)
                dve.wait_ge(vmax_all, b + 1)
                ops.tensor_scalar(vg[:, 0:1], emx[:, P:P + 1], 1e-30, None, ALU.max).then_inc(vscale, 1)
                dve.wait_ge(vscale, b * 4 + 1)
                ops.reciprocal(vg[:, 1:2], vg[:, 0:1]).then_inc(vscale, 1)
                dve.wait_ge(vscale, b * 4 + 2)
                ops.tensor_scalar(vg[:, 3:4], vg[:, 0:1], gam[:, 0:1], 1.0 / V_TOP, ALU.mult, ALU.mult).then_inc(vscale, 1)
                ops.tensor_scalar(vg[:, 2:3], vg[:, 1:2], V_TOP, None, ALU.mult).then_inc(vscale, 1)
                dve.wait_ge(vscale, b * 4 + 4)
                low_parts(b * (NB * JT), 0)
                low_parts(b * (NB * JT) + 1, 1)
                for q in range(VS):
                    js = slice(q * (JT // VS), (q + 1) * (JT // VS))
                    dve.wait_ge(vh_rdy, b * VS + (q + 1))
                    ops.scalar_tensor_tensor(vl[:, js, :], v32[:, js, :], vg[:, 2:3], vh[:, js, 0:C], ALU.mult,
                                             ALU.subtract).then_inc(vl_rdy, 1)

            def blk(b, n, c):
                g = b * NB + n
                s0 = g * JT
                more = c < NB - 1
                ups = {j: u for j, u, _, _, _, _ in up_pieces(b, n, c)}
                if more:
                    copy_queries(n + 1)
                for t in range(JT):
                    if more:
                        for u in EMAX_AT[t]:
                            row_max(g + 1, u)
                        if t == T_SHIFT:
                            shift(g + 1)
                        if t == T_MT + 1:
                            shift_rows(g + 1, n + 1)
                    if c > 0 and t in (T_OT[0] + 1, T_OT[1] + 1):
                        residual(g - 1, n - 1, T_OT.index(t - 1))
                    if t in T_ADD and T_ADD.index(t) in ups:
                        j = T_ADD.index(t)
                        add_piece(j, ups[j])
                    if t + 2 < JT or more:
                        low_parts(s0 + (t + 2), (t + 2) % JT)
                for it in range(IT):
                    if it < IT - 1:
                        dve.wait_ge(acc_rdy, g * (IT - 1) + (it + 1))
                    else:
                        dve.wait_ge(pv_done, s0 + JT)
                    ops.reciprocal(rl[:, it:it + 1], acc[it][:, C:C + 1]).then_inc(rl_rdy, 1)
                    dve.wait_ge(rl_rdy, g * IT + (it + 1))
                    ops.tensor_scalar(osb[:, it, :], acc[it][:, 0:C], rl[:, it:it + 1], vg[:, 3:4], ALU.mult,
                                      ALU.mult).then_inc(acc_free, 1)

            def leave(b):
                for half in range(2):
                    residual(b * NB + (NB - 1), NB - 1, half)

            walk(dve, enter, blk, leave)
            for j, u, _, _, _, _ in late_pieces():
                add_piece(j, u)

        @block.tensor
        def _(pe):
            mm = nc.tensor.matmul
            pe.wait_ge(wts_ld, 16 * 6)
            for i, nat in enumerate((osb[:, 0:2, :], osb[:, 2:4, :], hbuf[:, :, 0:C])):
                for h in range(CH):
                    for o in range(CH):
                        last = nc.tensor.transpose(acc[i][:, (h * CH + o) * P:(h * CH + o + 1) * P],
                                                   nat[:, o, h * P:(h + 1) * P], ident[:, :])
                last.then_inc(wt_rdy, 1)
            for i in range(2):
                for h in range(CH):
                    last = nc.tensor.transpose(acc[3][:, (i * CH + h) * D:(i * CH + h + 1) * D],
                                               hbuf[0:D, i, C + h * P:C + (h + 1) * P], ident[0:D, 0:D])
            last.then_inc(wt_rdy, 1)
            pe.wait_ge(wt_ok, 1)
            pe.wait_ge(mem_ok, 4)
            pe.wait_ge(memv_ok, 1)

            def max_unit(g, u):
                it, jc = divmod(u, JC)
                if u == 0:
                    pe.wait_ge(qm_rdy, g + 1)
                at_least(pe, emx_free, g * EU + u)
                mm(emx[:, :], qm[:, it * P:(it + 1) * P], ks[0:3 * D, jc * IB:(jc + 1) * IB], start=True,
                   stop=True).then_inc(emx_rdy, 1)

            def shift_transposes(g):
                pe.wait_ge(m_link, g * 4 + 4)
                for it in range(IT):
                    last = nc.tensor.transpose(wrk[0:2, it * P:(it + 1) * P], mhl[:, it, :].bitcast(F32), ident[:, :])
                last.then_inc(mt_rdy, 1)

            def energies(s, t, n):
                at_least(pe, pl_rdy, s - 1)
                mm(et[t % 2][:, :], ks[0:3 * D + 2, t * P:(t + 1) * P], qs[0:3 * D + 2, bass.ds(n * IB, IB)], start=True,
                   stop=True).then_inc(et_rdy, 1)

            def out_transposes(g, half):
                pe.wait_ge(acc_free, g * IT)
                if not half:
                    at_least(pe, y_rdy, g * 2 - 2)
                if half:
                    pe.wait_ge(ot_done, g * 2 - 1)
                for it in range(IT):
                    last = nc.tensor.transpose(wrk[:, it * P:(it + 1) * P], osb[:, it, half * P:(half + 1) * P], ident[:, :])
                last.then_inc(ot_rdy, 1)

            def conv2(chunk, half):
                pe.wait_ge(h_rdy, chunk * 2 + 2)
                if half:
                    pe.wait_ge(y_rdy, chunk * 2 + 1)
                for h in range(CH):
                    last = mm(wrk[:, :], w2t[:, h, half * P:(half + 1) * P], hbuf[:, h, :], start=h == 0, stop=h == CH - 1)
                last.then_inc(cv_rdy, 1)

            def enter(b):
                for u in range(2 * NB):
                    ck, oh = divmod(u, 2)
                    if oh == 0:
                        if isinstance(b, int) and b == 0:
                            pe.wait_ge(down_v, DN * V_PIECES * (ck + 1))
                            pe.wait_ge(down_p, DN * FIRST_POOL * (ck + 1))
                        else:
                            pe.wait_ge(down_p, down_count(b, PIECES * (ck + 1)))
                    if u < 4:
                        at_least(pe, acc_free, b * (NB * IT))
                    else:
                        pe.wait_ge(c1_done, b * (2 * NB) + (u - 3))
                    for h in range(CH):
                        last = mm(acc[u % 4][:, :], w1t[:, h, oh * P:(oh + 1) * P], xr_flat[:, h, ck * IB:(ck + 1) * IB],
                                  start=h == 0, stop=h == CH - 1)
                    last.then_inc(c1_rdy, 1)
                for ck in range(NB):
                    pe.wait_ge(c1_done, b * (2 * NB) + max(2 * ck + 2, 13 + ck if ck < 4 else 0))
                    if ck >= 4:
                        pe.wait_ge(qk_done, b * NB + (ck - 3))
                    for h in range(CH):
                        last = mm(acc[ck % 4][:, :], wqk[:, h, :], a[:, h, ck * IB:(ck + 1) * IB], start=h == 0,
                                  stop=h == CH - 1)
                    last.then_inc(qk_rdy, 1)
                for v in range(VU):
                    if v < 4:
                        pe.wait_ge(qk_done, b * NB + (v + 5))
                    else:
                        pe.wait_ge(v_done, b * VU + (v - 3))
                    for jj in range(VB):
                        jt = v * VB + jj
                        for h in range(CH):
                            last = mm(acc[v % 4][:, jj * C:(jj + 1) * C], a[:, h, jt * P:(jt + 1) * P], wvt[:, h, :],
                                      start=h == 0, stop=h == CH - 1)
                    last.then_inc(v_rdy, 1)
                    if v == 0:
                        pe.wait_ge(qk_done, b * NB + NB)
                    for u in (2 * v, 2 * v + 1):
                        max_unit(b * NB, u)
                at_least(pe, ot_done, b * (2 * NB))
                shift_transposes(b * NB)
                pe.wait_ge(vmax_1, b + 1)
                nc.tensor.transpose(emx[0:1, 0:P], vm1[:, :], ident[:, :]).then_inc(vmax_row, 1)
                pe.wait_ge(m_rdy, b * NB + 1)
                energies(b * (NB * JT), 0, 0)
                energies(b * (NB * JT) + 1, 1, 0)
                pe.wait_ge(vmax_one, b + 1)
                mm(emx[:, P:P + 1], ones[0:1, :], vma[0:1, 0:1], start=True, stop=True).then_inc(vmax_all, 1)

            def blk(b, n, c):
                g = b * NB + n
                s0 = g * JT
                more = c < NB - 1
                for t in range(JT):
                    pe.wait_ge(pl_rdy, s0 + (t + 1))
                    if t + 2 < JT:
                        energies(s0 + (t + 2), t + 2, n)
                    elif more:
                        if t + 2 == JT:
                            pe.wait_ge(m_rdy, g + 2)
                        energies(s0 + (t + 2), t + 2 - JT, n + 1)
                    if c == 0 and t % (JT // VS) == 0:
                        pe.wait_ge(vl_rdy, b * VS + (t // (JT // VS) + 1))
                    units = list(EMAX_AT[t]) if more else []
                    for it in range(IT):
                        if t == 0:
                            if c == 0:
                                pe.wait_ge(v_done, b * VU + VU)
                            else:
                                pe.wait_ge(acc_free, g * IT + (it - 3))
                        pt = slice(it * P, (it + 1) * P)
                        mm(acc[it][:, 0:C + 1], ph[:, t % 4, pt], vh[:, t, 0:C + 1], start=t == 0, stop=False)
                        mm(acc[it][:, 0:C], ph[:, t % 4, pt], vl[:, t, :], start=False, stop=False)
                        last = mm(acc[it][:, 0:C + 1], pl[:, t % 4, pt], vh[:, t, 0:C + 1], start=False, stop=t == JT - 1)
                        if it == IT - 1:
                            last.then_inc(pv_done, 1)
                        elif t == JT - 1:
                            last.then_inc(acc_rdy, 1)
                        if it in (1, 3) and units:
                            max_unit(g + 1, units.pop(0))
                    if c > 0 and t in T_OT:
                        out_transposes(g, T_OT.index(t))
                    if t in T_CV and not (isinstance(g, int) and g == 0):
                        conv2(g - 1, T_CV.index(t))
                    if more and t == T_MT:
                        at_least(pe, y_rdy, g * 2)
                        shift_transposes(g + 1)

            def leave(b):
                for half in range(2):
                    out_transposes(b * NB + NB, half)

            def batch(b):
                enter(b)
                blk(b, 0, 0)
                with pe.Fori(1, NB - 1) as n:
                    blk(b, n, 1)
                blk(b, NB - 1, NB - 1)
                leave(b)

            batch(0)
            with pe.Fori(1, B) as b:
                batch(b)
            for half in range(2):
                conv2(NB * B - 1, half)


N_PAR = 14
PAR_OPS = 3
EMAX_AT = []
_u = 0
for _t in range(JT):
    _k = min((2 if _t % 3 == 0 else 1), EU - _u)
    EMAX_AT.append(range(_u, _u + _k))
    _u += _k
assert _u == EU
T_SHIFT = 25
T_MT = 26
T_OT = (2, 6)
T_CV = (21, 23)
T_ADD = (7, 13, 19, 29)
T_RELU = (9, 15, 21, 31)


_INS = ['x', 'L0_conv_conv1_w', 'L0_conv_bn1_s', 'L0_conv_bn1_b', 'L0_conv_q_w', 'L0_conv_q_b', 'L0_conv_k_w',
        'L0_conv_k_b', 'L0_conv_v_w', 'L0_conv_v_b', 'L0_conv_att_gamma', 'L0_conv_bn2_s', 'L0_conv_bn2_b',
        'L0_conv_conv2_w', 'L0_conv_bn3_s', 'L0_conv_bn3_b']


def kernel(**inputs):
    import numpy as np
    import concourse.bacc as bacc
    from concourse.bass_utils import run_bass_kernel_spmd

    nc = bacc.Bacc("TRN2", target_bir_lowering=False, num_devices=1)
    arrays, args = {}, []

    def put(name, a):
        arrays[name] = a
        args.append(nc.dram_tensor(name, a.shape, mybir.dt.from_np(a.dtype), kind="ExternalInput").ap())

    for name in _INS:
        a = np.ascontiguousarray(inputs[name])
        put(f"in_{name}", a.reshape(1) if a.ndim == 0 else a)
    k = np.arange(S)
    put("identity", np.eye(P, dtype=np.float32))
    put("down_weights", (k / (S - 1)).astype(np.float32))
    put("up_weights", np.stack([-k / (H - 1), (S - 1 - k) / (H - 1)], axis=1).astype(np.float32))
    out = nc.dram_tensor("out", (B, C, H, H), F32, kind="ExternalOutput").ap()
    attention_block_kernel(nc, *args, out)
    r = run_bass_kernel_spmd(nc, [arrays], core_ids=[0])
    return r.results[0]["out"]
```

```python
import concourse.bass as bass
from concourse import mybir
from contextlib import ExitStack

F32 = mybir.dt.float32
F32R = mybir.dt.float32r
F16 = mybir.dt.float16
ACT = mybir.ActivationFunctionType
ALU = mybir.AluOpType
AX = mybir.AxisListType

B, C, H, D = 4, 256, 128, 32
S = H // 2
N = S * S
P = 128
CH = C // P
IB = 512
NB = N // IB
IT = IB // P
JT = N // P
JC = N // IB
EU = IT * JC
BR = IB // S
UR = 8
DR = 8
PIECES = 4
VB = 2
VU = JT // VB
VS = VU
VS_FIRST = 4
LOG_P = 8.0
V_TOP = 2.0 ** 14
BN = 1.0 / (1.0 + 1e-5) ** 0.5
DN, UP = 6, 5
FIRST_POOL = 2


def attention_block_kernel(nc, x, w1, s1, b1, wq, bq, wk, bk, wv, bv, gamma, s2, b2, w2, s3, b3,
                           ident_d, down_w, up_w, out):
    with ExitStack() as ctx:
        def sb(name, shape, dt=F32):
            return ctx.enter_context(nc.sbuf_tensor(name, shape, dt))

        def bank(name):
            return ctx.enter_context(nc.psum_tensor(name, [P, 512], F32))

        def sem(name):
            return ctx.enter_context(nc.semaphore(name))

        xv = sb("xv", [P, CH * N])
        xr = xv[:, :].rearrange("p (k h r c) -> p k h r c", h=CH, r=BR, c=S)
        xr_flat = xv[:, :].rearrange("p (k h n) -> p k h n", h=CH, n=IB)
        v32 = xv[:, :].rearrange("p (j c) -> p j c", c=C)
        a = sb("a", [P, CH, N])
        ks = sb("ks", [P, N], F32R)
        qs = sb("qs", [P, N], F32R)
        qm = sb("qm", [3 * D, IB], F32R)
        vh = sb("vh", [P, JT, C + 2], F16)
        vl = sb("vl", [P, JT, C], F16)
        ph = sb("ph", [P, 4, IB], F16)
        pl = sb("pl", [P, 4, IB], F16)
        osb = sb("osb", [P, IT, C])
        hbuf = sb("hbuf", [P, CH, IB])
        win = sb("win", [P, 2, CH, BR + 2, S])
        xres = sb("xres", [P, 4, UR, H])
        xin = sb("xin", [P, 2, DR, H])
        rd = sb("rd", [P, UR // 2 + 1, S])
        rt = sb("rt", [P, UR // 2, 2, S])
        y2 = sb("y2", [P, 2, UR, S])
        cd = sb("cd", [P, UR, S + 1])
        ct = sb("ct", [P, 2, UR, S, 2])
        dd = sb("dd", [P, DR // 2, S])
        w1t = sb("w1t", [P, CH, C])
        wvt = sb("wvt", [P, CH, C])
        w2t = sb("w2t", [P, CH, C])
        wqk = sb("wqk", [P, CH, 4 * D])
        ident = sb("ident", [P, P])
        dw = sb("dw", [P, S])
        uw = sb("uw", [P, S, 2])
        par = sb("par", [P, 8, CH])
        S1, B1, S2, B2, S3, B3, BV = range(7)
        gam = sb("gam", [P, 1])
        qkb = sb("qkb", [P, 1])
        mx = sb("mx", [P, IT, JC])
        m4 = sb("m4", [P, IT])
        mn = sb("mn", [P, IT])
        mhl = sb("mhl", [P, IT, 2], F32R)
        vmx = sb("vmx", [P, VU])
        vm1 = sb("vm1", [P, 1])
        vma = sb("vma", [1, 1])
        ones = sb("ones", [1, P])
        vg = sb("vg", [P, 4])
        rl = sb("rl", [P, IT])

        acc = [bank(f"acc{i}") for i in range(IT)]
        et = [bank(f"et{i}") for i in range(2)]
        emx = bank("emx")
        wrk = bank("wrk")

        par_ld, wts_ld = sem("par_ld"), sem("wts_ld")
        par_ok, wt_rdy, wt_ok, mem_ok, memv_ok = (sem(n) for n in ("par_ok", "wt_rdy", "wt_ok", "mem_ok", "memv_ok"))
        xin_ld = [sem(f"xin_ld{i}") for i in range(2)]
        xres_ld = [sem(f"xres_ld{i}") for i in range(4)]
        stored = [sem(f"stored{i}") for i in range(4)]
        down_p, down_v = sem("down_p"), sem("down_v")
        up_p, up_v = sem("up_p"), sem("up_v")
        up_added, up_relu = sem("up_added"), sem("up_relu")
        c1_rdy, c1_done = sem("c1_rdy"), sem("c1_done")
        qk_rdy, qk_hi, qk_done = sem("qk_rdy"), sem("qk_hi"), sem("qk_done")
        v_rdy, v_done, vmax_part, vmax_1 = (sem(n) for n in ("v_rdy", "v_done", "vmax_part", "vmax_1"))
        vmax_row, vmax_one, vmax_all = sem("vmax_row"), sem("vmax_one"), sem("vmax_all")
        vscale, vh_rdy, vl_rdy = sem("vscale"), sem("vh_rdy"), sem("vl_rdy")
        qm_rdy, emx_rdy, emx_free, m_link, mt_rdy, m_rdy = (
            sem(n) for n in ("qm_rdy", "emx_rdy", "emx_free", "m_link", "mt_rdy", "m_rdy"))
        et_rdy, p_rdy, pl_rdy, pv_done = sem("et_rdy"), sem("p_rdy"), sem("pl_rdy"), sem("pv_done")
        acc_rdy, rl_rdy, acc_out, acc_out_v = sem("acc_rdy"), sem("rl_rdy"), sem("acc_out"), sem("acc_out_v")
        ot_rdy, ot_done, h_rdy = sem("ot_rdy"), sem("ot_done"), sem("h_rdy")
        cv_rdy, y_rdy = sem("cv_rdy"), sem("y_rdy")

        def at_least(eng, s, value):
            if isinstance(value, int) and value <= 0:
                return
            eng.wait_ge(s, value)

        def walk(eng, enter, block, leave, last_apart=False):
            def batch(b):
                enter(b)
                for n in range(3):
                    block(b, n, n)
                with eng.Fori(0, (NB - 4) // 2) as i:
                    block(b, i * 2 + 3, 3)
                    block(b, i * 2 + 4, 4)
                block(b, NB - 1, NB - 1)
                leave(b)

            batch(0)
            if last_apart:
                with eng.Fori(1, B - 1) as b:
                    batch(b)
                batch(B - 1)
            else:
                with eng.Fori(1, B) as b:
                    batch(b)

        def held(eng, value):
            return value if isinstance(value, int) else eng.snap(value)

        def up_pieces(b, n, c):
            for j in range(PIECES):
                back = 3 if j < 3 else 2
                g = b * NB + n
                if isinstance(g, int) and g < back:
                    continue
                wrap = c < back
                yield (j, g * PIECES - 11 + j, b - 1 if wrap else b, n + NB - back if wrap else n - back,
                       (c - back) % 2, (1 + j) % PIECES)

        LAST_PIECES = range(PIECES * (NB * B - 1) - 11 + PIECES, PIECES * NB * B)

        def late_pieces():
            for u in LAST_PIECES:
                chunk = u // PIECES
                yield (u + 3) % 4, u, B - 1, chunk - (B - 1) * NB, chunk % 2, u % PIECES

        def xslot(j):
            return (j + 1) % 4

        def piece_rows(n, k):
            return k % 2, (n * (2 * BR) + (k // 2) * UR)

        def dram_rows(t, b, half, row, rows):
            v = t[bass.ds(b, 1), half * P:(half + 1) * P, bass.ds(row, rows), :]
            return v.rearrange("o p r c -> (o p) r c")

        V_PIECES = PIECES - FIRST_POOL
        XRES_FIRST = NB * V_PIECES // 4
        POOL_FIRST = DN * NB * FIRST_POOL

        def down_count(b, d):
            return (b - 1) * (DN * NB * PIECES) + (POOL_FIRST + DN * d)

        nc.disable_value_cache = True
        block = ctx.enter_context(nc.Block())

        @block.sync
        def _(sp):
            npar = 0
            for i, t in ((S1, s1), (B1, b1), (S2, s2), (B2, b2), (S3, s3), (B3, b3), (BV, bv)):
                sp.dma_start(par[:, i, :], t.rearrange("(h p) -> p h", p=P), allow_slow_non_contiguous=True).then_inc(par_ld, 16)
                npar += 1
            for i, t in enumerate((bk, bk, bq, bq)):
                sp.dma_start(qkb[i * D:(i + 1) * D, :], t.unsqueeze(1)).then_inc(par_ld, 16)
                npar += 1
            sp.dma_start(gam[:], gamma.partition_broadcast(P)).then_inc(par_ld, 16)
            sp.dma_start(dw[:], down_w.partition_broadcast(P)).then_inc(par_ld, 16)
            sp.dma_start(uw[:], up_w.partition_broadcast(P)).then_inc(par_ld, 16)
            assert npar + 3 == N_PAR

            for d in range(NB * PIECES):
                ck, j = divmod(d, PIECES)
                if d == 2:
                    sp.dma_start(ident[:], ident_d).then_inc(wts_ld, 16)
                    for dst, t in ((osb[:, 0:2, :], w1), (osb[:, 2:4, :], wv), (hbuf[:, :, 0:C], w2)):
                        sp.dma_start(dst, t.rearrange("(o p) c -> p o c", p=P)).then_inc(wts_ld, 16)
                    sp.dma_start(hbuf[0:D, 0, C:2 * C], wk).then_inc(wts_ld, 16)
                    sp.dma_start(hbuf[0:D, 1, C:2 * C], wq).then_inc(wts_ld, 16)
                src = dram_rows(x, 0, j % 2, (2 * ck + j // 2) * DR, DR)
                if j < V_PIECES:
                    i = ck * V_PIECES + j
                    at_least(sp, down_v, DN * (i - 3))
                    sp.dma_start(xres[:, i % 4], src).then_inc(xres_ld[i % 4], 16)
                else:
                    i = ck * FIRST_POOL + j - V_PIECES
                    at_least(sp, down_p, DN * (i - 1))
                    sp.dma_start(xin[:, i % 2], src).then_inc(xin_ld[i % 2], 16)

            def load_shortcut(j, u, b, n, k):
                half, row = piece_rows(n, k)
                s = xslot(j)
                uses = (u - s) // 4 if isinstance(u, int) else None
                at_least(sp, stored[s], (u - s) * 4 if uses is None else uses * 16)
                if isinstance(u, int) and u < 4:
                    sp.wait_ge(down_v, DN * NB * V_PIECES)
                sp.dma_start(xres[:, s], dram_rows(x, b, half, row, UR)).then_inc(xres_ld[s], 16)

            def enter(b):
                pass

            def blk(b, n, c):
                ups = {j: (u, ub, un, k) for j, u, ub, un, _, k in up_pieces(b, n, c)}
                for j in range(PIECES):
                    if not (isinstance(b, int) and b == B - 1):
                        i = n * PIECES + j
                        sp.wait_ge(down_p, down_count(b + 1, i - 1))
                        sp.dma_start(xin[:, j % 2], dram_rows(x, b + 1, j % 2, (n * 2 + j // 2) * DR, DR)).then_inc(
                            xin_ld[j % 2], 16)
                    if j in ups:
                        load_shortcut(j, *ups[j])

            def leave(b):
                pass

            walk(sp, enter, blk, leave, last_apart=True)
            for j, u, ub, un, _, k in late_pieces():
                load_shortcut(j, u, ub, un, k)
            for s in range(4):
                sp.wait_ge(stored[s], 16 * B * NB)

        def down_piece(eng, ops, s, count, src, tmp, dst, first_small_row):
            pair = src.rearrange("p (r two) c -> p r two c", two=2)
            even, odd = pair[:, :, 0, :], pair[:, :, 1, :]
            rw = dw[:, bass.ds(first_small_row, DR // 2)].unsqueeze(2).broadcast_to([P, DR // 2, H])
            cw = dw[:, :].unsqueeze(1).broadcast_to([P, DR // 2, S])
            cols = even.rearrange("p r (c two) -> p r c two", two=2)
            ops.tensor_tensor(odd, odd, even, ALU.subtract).then_inc(s, 1)
            eng.wait_ge(s, count + 1)
            ops.tensor_tensor(odd, odd, rw, ALU.mult).then_inc(s, 1)
            eng.wait_ge(s, count + 2)
            ops.tensor_tensor(even, even, odd, ALU.add).then_inc(s, 1)
            eng.wait_ge(s, count + 3)
            ops.tensor_tensor(tmp, cols[:, :, :, 1], cols[:, :, :, 0], ALU.subtract).then_inc(s, 1)
            eng.wait_ge(s, count + 4)
            ops.tensor_tensor(tmp, tmp, cw, ALU.mult).then_inc(s, 1)
            eng.wait_ge(s, count + 5)
            ops.tensor_tensor(dst, cols[:, :, :, 0], tmp, ALU.add).then_inc(s, 1)

        @block.gpsimd
        def _(pool):
            ops = nc.gpsimd
            ops.memset(ks[3 * D:P, :].bitcast(F32), 1.0).then_inc(mem_ok, 1)
            pool.wait_ge(mem_ok, 1)
            ops.memset(vh[:, :, C:C + 2], 1.0).then_inc(mem_ok, 1)
            pool.wait_ge(mem_ok, 2)
            ops.memset(ones[:], 1.0).then_inc(mem_ok, 1)
            pool.wait_ge(mem_ok, 3)
            ops.memset(cd[:], 0.0).then_inc(mem_ok, 1)
            pool.wait_ge(mem_ok, 4)
            pool.wait_ge(par_ld, 16 * N_PAR)
            for i in range(NB * FIRST_POOL):
                ck, j = divmod(i, FIRST_POOL)
                j += V_PIECES
                pool.wait_ge(xin_ld[i % 2], 16 * (i // 2 + 1))
                small = (2 * ck + j // 2) * (DR // 2)
                down_piece(pool, ops, down_p, DN * i, xin[:, i % 2], dd[:],
                           xr[:, ck, j % 2, (j // 2) * (DR // 2):(j // 2 + 1) * (DR // 2), :], small)

            def up_piece(u, n, par_, k, y2, ct):
                half, q = k % 2, k // 2
                w = win[:, par_, half, q * (BR // 2):q * (BR // 2) + BR // 2 + 2, :]
                R = UR // 2
                base = u * UP
                ops.tensor_tensor(rd[:], w[:, 1:R + 2, :], w[:, 0:R + 1, :], ALU.subtract).then_inc(up_p, 1)
                pool.wait_ge(up_p, base + 1)
                first = n * BR + q * R
                for parity in range(2):
                    wt = uw[:, bass.ds(first, R), parity:parity + 1].broadcast_to([P, R, S])
                    last = ops.tensor_tensor(rt[:, :, parity, :], rd[:, parity:parity + R, :], wt, ALU.mult)
                last.then_inc(up_p, 1)
                pool.wait_ge(up_p, base + 2)
                at_least(pool, up_added, u * 2 - 2)
                mid = w[:, 1:R + 1, :].unsqueeze(2).broadcast_to([P, R, 2, S])
                ops.tensor_tensor(y2.rearrange("p (r two) c -> p r two c", two=2), mid, rt[:], ALU.add).then_inc(up_p, 1)
                pool.wait_ge(up_p, base + 3)
                ops.tensor_tensor(cd[:, :, 1:S], y2[:, :, 1:S], y2[:, :, 0:S - 1], ALU.subtract).then_inc(up_p, 1)
                pool.wait_ge(up_p, base + 4)
                for parity in range(2):
                    wt = uw[:, :, parity].unsqueeze(1).broadcast_to([P, UR, S])
                    last = ops.tensor_tensor(ct[:, :, :, parity], cd[:, :, parity:parity + S], wt, ALU.mult)
                last.then_inc(up_p, 1)

            def enter(b):
                pass

            def blk(b, n, c):
                ups = {j: (u, un, pr, k) for j, u, _, un, pr, k in up_pieces(b, n, c)}
                g = b * NB + n
                for j in range(PIECES):
                    if j in ups:
                        if j == 3:
                            pool.wait_ge(y_rdy, g * 2)
                        up_piece(*ups[j], y2[:, (j + 1) % 2], ct[:, (j + 1) % 2])
                    if not (isinstance(b, int) and b == B - 1):
                        if j == 0:
                            pool.wait_ge(vl_rdy, b * VS + n * (VS // NB) + VS // NB)
                        i = n * PIECES + j
                        fills = NB * FIRST_POOL // 2
                        pool.wait_ge(xin_ld[j % 2], b * (16 * NB * PIECES // 2) + n * 32 + (16 * (fills + j // 2 + 1)))
                        small = (n * 2 + j // 2) * (DR // 2)
                        dst = xr[:, bass.ds(n, 1), j % 2, (j // 2) * (DR // 2):(j // 2 + 1) * (DR // 2), :]
                        down_piece(pool, ops, down_p, down_count(b + 1, i), xin[:, j % 2], dd[:],
                                   dst.rearrange("p o r c -> p (o r) c"), small)

            def leave(b):
                pass

            walk(pool, enter, blk, leave, last_apart=True)
            for j, u, ub, un, pr, k in late_pieces():
                if k == 0 and un == NB - 2:
                    pool.wait_ge(y_rdy, 2 * NB * B)
                up_piece(u, un, pr, k, y2[:, u % 2], ct[:, u % 2])

        @block.scalar
        def _(act):
            ops = nc.scalar

            def weights_of(s, t):
                act.wait_ge(et_rdy, s + 1)
                at_least(act, pv_done, s - 3)
                ops.activation(ph[:, t % 4, :], et[t % 2][:, :], ACT.Exp)
                ops.activation(et[t % 2][:, :], et[t % 2][:, :], ACT.Exp).then_inc(p_rdy, 1)

            def relu_h(chunk, half):
                act.wait_ge(ot_done, chunk * 2 + (half + 1))
                ops.activation(hbuf[:, half, :], hbuf[:, half, :], ACT.Relu, bias=par[:, B2, half:half + 1],
                               scale=par[:, S2, half:half + 1]).then_inc(h_rdy, 1)

            def bn3(chunk, par_, half, first, last):
                act.wait_ge(cv_rdy, chunk * 2 + (half + 1))
                if half == 0:
                    at_least(act, up_p, (chunk - 1) * (UP * PIECES))
                    at_least(act, y_rdy, chunk * 2)
                new, old = win[:, par_, half], win[:, 1 - par_, half]
                cv = wrk[:, :].rearrange("p (r c) -> p r c", c=S)
                jobs = [(new[:, 0:1, :], cv[:, 0:1, :])] if first else [(old[:, BR + 1:BR + 2, :], cv[:, 0:1, :])]
                if last:
                    jobs.append((new[:, BR + 1:BR + 2, :], cv[:, BR - 1:BR, :]))
                if not first:
                    ops.copy(new[:, 0, :], old[:, BR, :])
                for dst, src in jobs + [(new[:, 1:BR + 1, :], cv)]:
                    done = ops.activation(dst, src, ACT.Identity, bias=par[:, B3, half:half + 1], scale=par[:, S3, half:half + 1])
                done.then_inc(y_rdy, 1)

            def final_relu(j, u):
                act.wait_ge(up_added, u * 2 + 2)
                ops.activation(xres[:, xslot(j)], xres[:, xslot(j)], ACT.Relu).then_inc(up_relu, 1)

            def store(j, u, b, n, k):
                half, row = piece_rows(n, k)
                act.wait_ge(up_relu, u + 1)
                act.dma_start(dram_rows(out, b, half, row, UR), xres[:, xslot(j)]).then_inc(stored[xslot(j)], 16)

            act.wait_ge(par_ok, PAR_OPS)

            def conv1_out(b, ck, oh):
                u = 2 * ck + oh
                act.wait_ge(c1_rdy, b * (2 * NB) + (u + 1))
                ops.activation(a[:, oh, ck * IB:(ck + 1) * IB], acc[bank_of("conv1", u)][:, :], ACT.Relu,
                               bias=par[:, B1, oh:oh + 1], scale=par[:, S1, oh:oh + 1]).then_inc(c1_done, 1)

            def qk_high(b, ck):
                cs = slice(ck * IB, (ck + 1) * IB)
                act.wait_ge(qk_rdy, b * NB + (ck + 1))
                ps = acc[bank_of("qk", ck)]
                ops.activation(ks[0:2 * D, cs], ps[0:2 * D, :], ACT.Identity, bias=qkb[0:2 * D, :])
                ops.activation(qs[0:2 * D, cs], ps[2 * D:4 * D, :], ACT.Identity, bias=qkb[2 * D:4 * D, :])
                ops.activation(qs[2 * D:3 * D, cs], ps[2 * D:3 * D, :], ACT.Identity,
                               bias=qkb[2 * D:3 * D, :]).then_inc(qk_hi, 1)

            def values_out(b, v):
                act.wait_ge(v_rdy, b * VU + (v + 1))
                ops.activation(v32[:, v * VB:(v + 1) * VB, :], acc[bank_of("values", v)][:, :].rearrange("p (j c) -> p j c", c=C),
                               ACT.Copy).then_inc(v_done, 1)

            def values_high(b, q):
                js = slice(q * (JT // VS), (q + 1) * (JT // VS))
                ops.activation(vh[:, js, 0:C], v32[:, js, :], ACT.Copy, scale=vg[:, 2:3]).then_inc(vh_rdy, 1)

            def enter(b):
                at_least(act, ot_done, b * (2 * NB))
                for kind, i in SEQUENCE:
                    if kind == "conv1":
                        conv1_out(b, i // 2, i % 2)
                    elif kind == "qk":
                        qk_high(b, i)
                    elif kind == "values":
                        values_out(b, i)
                weights_of(b * (NB * JT), 0)
                weights_of(b * (NB * JT) + 1, 1)
                act.wait_ge(vscale, b * 4 + 4)
                for q in range(VS_FIRST):
                    values_high(b, q)

            def blk(b, n, c):
                g = held(act, b * NB + n)
                s0 = held(act, g * JT)
                ups = {j: (u, ub, un, k) for j, u, ub, un, _, k in up_pieces(b, n, c)}
                before = {}
                if not (isinstance(g, int) and g < 3):
                    before = {j: (u, ub, un, k) for j, u, ub, un, _, k in
                              (up_pieces(b, n - 1, c - 1) if c else up_pieces(b - 1, NB - 1, NB - 1))}
                for t in range(JT):
                    if c > 0 and t in (T_OT[0] + 2, T_OT[1] + 2):
                        relu_h(g - 1, T_OT.index(t - 2))
                    if t in (T_CV[0] + 1, T_CV[1] + 1) and not (isinstance(g, int) and g == 0):
                        bn3(g - 1, (c - 1) % 2, T_CV.index(t - 1), c == 1, c == 0)
                    if t in T_RELU[0:3] and T_RELU.index(t) in ups:
                        j = T_RELU.index(t)
                        final_relu(j, ups[j][0])
                    if t - 1 in T_RELU[0:3] and T_RELU.index(t - 1) in ups:
                        j = T_RELU.index(t - 1)
                        store(j, *ups[j])
                    if t == T_RELU[3] and 3 in before:
                        final_relu(3, before[3][0])
                    if t == T_RELU[3] + 1 and 3 in before:
                        store(3, *before[3])
                    if t + 2 < JT or c < NB - 1:
                        weights_of(s0 + (t + 2), (t + 2) % JT)
                    if c == 0 and t + VS_FIRST < VS:
                        values_high(b, t + VS_FIRST)
                for it in range(IT - 1):
                    act.wait_ge(rl_rdy, g * IT + (it + 1))
                    ops.activation(osb[:, it, :], acc[it][:, 0:C], ACT.Copy, scale=rl[:, it:it + 1]).then_inc(acc_out, 1)

            def leave(b):
                g1 = b * NB + NB
                for half in range(2):
                    relu_h(g1 - 1, half)

            walk(act, enter, blk, leave)
            j, u, ub, un, _, k = list(up_pieces(B - 1, NB - 1, NB - 1))[3]
            final_relu(j, u)
            store(j, u, ub, un, k)
            for j, u, ub, un, _, k in late_pieces():
                if k == 0 and un == NB - 2:
                    for half in range(2):
                        bn3(NB * B - 1, (NB - 1) % 2, half, False, True)
                final_relu(j, u)
                store(j, u, ub, un, k)

        @block.vector
        def _(dve):
            ops = nc.vector
            ops.memset(qs[3 * D:P, :].bitcast(F32), 0.0).then_inc(memv_ok, 1)
            dve.wait_ge(par_ld, 16 * N_PAR)
            for i in (S1, S2, S3):
                ops.tensor_scalar(par[:, i, :], par[:, i, :], BN, None, ALU.mult)
            ops.tensor_scalar(par[:, BV, :], par[:, BV, :], gam[:, 0:1], None, ALU.mult).then_inc(par_ok, 1)
            dve.wait_ge(par_ok, 1)
            ops.tensor_tensor(par[:, BV, :], par[:, BV, :], par[:, S2, :], ALU.mult).then_inc(par_ok, 1)
            dve.wait_ge(par_ok, 2)
            ops.tensor_tensor(par[:, B2, :], par[:, B2, :], par[:, BV, :], ALU.add).then_inc(par_ok, 1)

            def transposed_weights():
                for i, dst in enumerate((w1t, wvt, w2t)):
                    dve.wait_ge(wt_rdy, i + 1)
                    ops.tensor_copy(dst[:].rearrange("p h c -> p (h c)"), acc[i][:, :])
                dve.wait_ge(wt_rdy, 4)
                for i in range(4):
                    last = ops.tensor_copy(wqk[:, :, i * D:(i + 1) * D],
                                           acc[3][:, 0:4 * D].rearrange("p (w h d) -> p w h d", w=2, h=CH)[:, i // 2])
                last.then_inc(wt_ok, 1)

            def first_down(ck):
                for j in range(V_PIECES):
                    i = ck * V_PIECES + j
                    dve.wait_ge(xres_ld[i % 4], 16 * (i // 4 + 1))
                    small = (2 * ck + j // 2) * (DR // 2)
                    down_piece(dve, ops, down_v, DN * i, xres[:, i % 4], rt[:, :, 0, :],
                               xr[:, ck, j % 2, (j // 2) * (DR // 2):(j // 2 + 1) * (DR // 2), :], small)

            first_down(0)
            transposed_weights()
            first_down(1)

            def row_max(g, u, bank):
                dve.wait_ge(emx_rdy, g * EU + (u + 1))
                ops.reduce_max(mx[:, u % IT, u // IT:u // IT + 1], bank[:, :], AX.X).then_inc(emx_free, 1)

            def shift(g):
                dve.wait_ge(emx_free, g * EU + EU)
                ops.reduce_max(m4[:], mx[:], AX.X).then_inc(m_link, 1)
                dve.wait_ge(m_link, g * 4 + 1)
                ops.tensor_scalar(mn[:], m4[:], -1.0, LOG_P, ALU.mult, ALU.add).then_inc(m_link, 1)
                dve.wait_ge(m_link, g * 4 + 2)
                ops.tensor_copy(mhl[:, :, 0], mn[:]).then_inc(m_link, 1)
                dve.wait_ge(m_link, g * 4 + 3)
                ops.tensor_tensor(mhl[:, :, 1], mn[:], mhl[:, :, 0].bitcast(F32), ALU.subtract).then_inc(m_link, 1)

            def shift_rows(g, n):
                dve.wait_ge(mt_rdy, g + 1)
                ops.tensor_copy(qs[3 * D:3 * D + 2, bass.ds(n * IB, IB)], wrk[0:2, :]).then_inc(m_rdy, 1)

            def low_parts(s, t):
                dve.wait_ge(p_rdy, s + 1)
                at_least(dve, pv_done, s - 3)
                ops.tensor_tensor(pl[:, t % 4, :], et[t % 2][:, :], ph[:, t % 4, :], ALU.subtract).then_inc(pl_rdy, 1)

            def copy_queries(n):
                ops.tensor_copy(qm[:, :], qs[0:3 * D, bass.ds(n * IB, IB)].bitcast(F32)).then_inc(qm_rdy, 1)

            def residual(chunk, n, half):
                dve.wait_ge(ot_rdy, chunk * 2 + (half + 1))
                at_least(dve, cv_rdy, chunk * 2)
                ops.scalar_tensor_tensor(hbuf[:, half, :], wrk[:, :], vg[:, 3:4], a[:, half, bass.ds(n * IB, IB)], ALU.mult,
                                         ALU.add).then_inc(ot_done, 1)

            def add_piece(j, u, part):
                rs = slice((part % 2) * (UR // 2), (part % 2 + 1) * (UR // 2))
                xs = xres[:, xslot(j), rs, :]
                if part == 0:
                    dve.wait_ge(up_p, u * UP + UP)
                    dve.wait_ge(xres_ld[xslot(j)], (u - xslot(j)) * 4 + 16 * (XRES_FIRST + 1))
                if part < 2:
                    ops.tensor_tensor(xs, xs, ct[:, (j + 1) % 2, rs].rearrange("p r c two -> p r (c two)"), ALU.add).then_inc(up_v, 1)
                else:
                    dve.wait_ge(up_v, u * 2 + (part - 1))
                    xs4 = xs.rearrange("p r (c two) -> p r c two", two=2)
                    ops.tensor_tensor(xs4, xs4, y2[:, (j + 1) % 2, rs].unsqueeze(3).broadcast_to([P, UR // 2, S, 2]),
                                      ALU.add).then_inc(up_added, 1)

            def qk_low(b, ck):
                cs = slice(ck * IB, (ck + 1) * IB)
                dve.wait_ge(qk_hi, b * NB + (ck + 1))
                ps = acc[bank_of("qk", ck)]
                ops.tensor_copy(ks[2 * D:3 * D, cs], ks[0:D, cs].bitcast(F32))
                for t, r in ((ks, slice(D, 2 * D)), (qs, slice(2 * D, 3 * D))):
                    last = ops.scalar_tensor_tensor(t[r, cs], ps[r, :], qkb[r, :], t[r, cs].bitcast(F32), ALU.add, ALU.subtract)
                last.then_inc(qk_done, 1)
                if ck == 0:
                    dve.wait_ge(qk_done, b * NB + 1)
                    copy_queries(0)

            def value_max(b, v):
                dve.wait_ge(v_done, b * VU + (v + 1))
                ops.tensor_reduce(vmx[:, v:v + 1], v32[:, v * VB:(v + 1) * VB, :], AX.XY, ALU.max,
                                  apply_absolute_value=True).then_inc(vmax_part, 1)

            def values_low(b, q):
                js = slice(q * (JT // VS), (q + 1) * (JT // VS))
                dve.wait_ge(vh_rdy, b * VS + (q + 1))
                ops.scalar_tensor_tensor(vl[:, js, :], v32[:, js, :], vg[:, 2:3], vh[:, js, 0:C], ALU.mult,
                                         ALU.subtract).then_inc(vl_rdy, 1)

            def enter(b):
                for kind, i in SEQUENCE:
                    if kind == "conv1" and i % 2 == 0 and isinstance(b, int) and i // 2 + 2 < NB:
                        first_down(i // 2 + 2)
                    elif kind == "qk":
                        qk_low(b, i)
                    elif kind == "max":
                        row_max(b * NB, i, (emx, *et)[i % 3])
                    elif kind == "values":
                        value_max(b, i)
                    if (kind, i) == SHIFT_AFTER:
                        shift(b * NB)
                dve.wait_ge(vmax_part, b * VU + VU)
                ops.reduce_max(vm1[:], vmx[:], AX.X).then_inc(vmax_1, 1)
                shift_rows(b * NB, 0)
                dve.wait_ge(vmax_row, b + 1)
                ops.reduce_max(vma[:], emx[0:1, 0:P], AX.X).then_inc(vmax_one, 1)
                dve.wait_ge(vmax_all, b + 1)
                ops.tensor_scalar(vg[:, 0:1], emx[:, P:P + 1], 1e-30, None, ALU.max).then_inc(vscale, 1)
                dve.wait_ge(vscale, b * 4 + 1)
                ops.reciprocal(vg[:, 1:2], vg[:, 0:1]).then_inc(vscale, 1)
                ops.tensor_scalar(vg[:, 3:4], vg[:, 0:1], gam[:, 0:1], 1.0 / V_TOP, ALU.mult, ALU.mult).then_inc(vscale, 1)
                dve.wait_ge(vscale, b * 4 + 2)
                ops.tensor_scalar(vg[:, 2:3], vg[:, 1:2], V_TOP, None, ALU.mult).then_inc(vscale, 1)
                dve.wait_ge(vscale, b * 4 + 4)
                low_parts(b * (NB * JT), 0)
                low_parts(b * (NB * JT) + 1, 1)
                for q in range(VS_FIRST):
                    values_low(b, q)

            def row_sum(g, it):
                if it < IT - 1:
                    dve.wait_ge(acc_rdy, g * (IT - 1) + (it + 1))
                else:
                    dve.wait_ge(pv_done, g * JT + JT)
                ops.reciprocal(rl[:, it:it + 1], acc[it][:, C:C + 1]).then_inc(rl_rdy, 1)

            def blk(b, n, c):
                g = held(dve, b * NB + n)
                s0 = held(dve, g * JT)
                more = c < NB - 1
                ups = {j: u for j, u, _, _, _, _ in up_pieces(b, n, c)}
                if more:
                    copy_queries(n + 1)
                for t in range(JT):
                    if more:
                        if t == T_SHIFT:
                            shift(g + 1)
                        if t == T_MT + 1:
                            shift_rows(g + 1, n + 1)
                        for u in EMAX_AT[t]:
                            row_max(g + 1, u, emx)
                    if c > 0 and t in (T_OT[0] + 1, T_OT[1] + 1):
                        residual(g - 1, n - 1, T_OT.index(t - 1))
                    for j in ups:
                        if t in T_ADD[j]:
                            add_piece(j, ups[j], T_ADD[j].index(t))
                    if t == JT - 1:
                        for it in range(IT - 1):
                            row_sum(g, it)
                    if t + 2 < JT or more:
                        low_parts(s0 + (t + 2), (t + 2) % JT)
                    if c == 0 and t + VS_FIRST < VS:
                        values_low(b, t + VS_FIRST)
                row_sum(g, IT - 1)
                dve.wait_ge(rl_rdy, g * IT + IT)
                ops.tensor_scalar(osb[:, IT - 1, :], acc[IT - 1][:, 0:C], rl[:, IT - 1:IT], None, ALU.mult).then_inc(acc_out_v, 1)

            def leave(b):
                for half in range(2):
                    residual(b * NB + (NB - 1), NB - 1, half)

            walk(dve, enter, blk, leave)
            for j, u, _, _, _, _ in late_pieces():
                for part in range(4):
                    add_piece(j, u, part)

        @block.tensor
        def _(pe):
            mm = nc.tensor.matmul
            pe.wait_ge(wts_ld, 16 * 6)
            for i, nat in enumerate((osb[:, 0:2, :], osb[:, 2:4, :], hbuf[:, :, 0:C])):
                for h in range(CH):
                    for o in range(CH):
                        last = nc.tensor.transpose(acc[i][:, (h * CH + o) * P:(h * CH + o + 1) * P],
                                                   nat[:, o, h * P:(h + 1) * P], ident[:, :])
                last.then_inc(wt_rdy, 1)
            for i in range(2):
                for h in range(CH):
                    last = nc.tensor.transpose(acc[3][:, (i * CH + h) * D:(i * CH + h + 1) * D],
                                               hbuf[0:D, i, C + h * P:C + (h + 1) * P], ident[0:D, 0:D])
            last.then_inc(wt_rdy, 1)
            pe.wait_ge(wt_ok, 1)
            pe.wait_ge(mem_ok, 4)
            pe.wait_ge(memv_ok, 1)

            def max_unit(g, u, bank, before):
                jc, it = divmod(u, IT)
                if u == 0:
                    pe.wait_ge(qm_rdy, g + 1)
                at_least(pe, emx_free, g * EU + (u + 1 - before))
                mm(bank[:, :], qm[:, it * P:(it + 1) * P], ks[0:3 * D, jc * IB:(jc + 1) * IB], start=True,
                   stop=True).then_inc(emx_rdy, 1)

            def shift_transposes(g):
                pe.wait_ge(m_link, g * 4 + 4)
                for it in range(IT):
                    last = nc.tensor.transpose(wrk[0:2, it * P:(it + 1) * P], mhl[:, it, :].bitcast(F32), ident[:, :])
                last.then_inc(mt_rdy, 1)

            def energies(s, t, n):
                at_least(pe, pl_rdy, s - 1)
                mm(et[t % 2][:, :], ks[0:3 * D + 2, t * P:(t + 1) * P], qs[0:3 * D + 2, bass.ds(n * IB, IB)], start=True,
                   stop=True).then_inc(et_rdy, 1)

            def out_transposes(g, half):
                pe.wait_ge(acc_out, g * (IT - 1))
                pe.wait_ge(acc_out_v, g)
                if not half:
                    at_least(pe, y_rdy, g * 2 - 2)
                if half:
                    pe.wait_ge(ot_done, g * 2 - 1)
                for it in range(IT):
                    last = nc.tensor.transpose(wrk[:, it * P:(it + 1) * P], osb[:, it, half * P:(half + 1) * P], ident[:, :])
                last.then_inc(ot_rdy, 1)

            def conv2(chunk, half):
                pe.wait_ge(h_rdy, chunk * 2 + 2)
                if half:
                    pe.wait_ge(y_rdy, chunk * 2 + 1)
                for h in range(CH):
                    last = mm(wrk[:, :], w2t[:, h, half * P:(half + 1) * P], hbuf[:, h, :], start=h == 0, stop=h == CH - 1)
                last.then_inc(cv_rdy, 1)

            def conv1(b, ck, oh):
                if oh == 0:
                    if isinstance(b, int):
                        pe.wait_ge(down_v, DN * V_PIECES * (ck + 1))
                        pe.wait_ge(down_p, DN * FIRST_POOL * (ck + 1))
                    else:
                        pe.wait_ge(down_p, down_count(b, PIECES * (ck + 1)))
                for h in range(CH):
                    last = mm(acc[bank_of("conv1", 2 * ck + oh)][:, :], w1t[:, h, oh * P:(oh + 1) * P], xr_flat[:, ck, h, :],
                              start=h == 0, stop=h == CH - 1)
                last.then_inc(c1_rdy, 1)

            def qk(b, ck):
                pe.wait_ge(c1_done, b * (2 * NB) + (2 * ck + 2))
                for h in range(CH):
                    last = mm(acc[bank_of("qk", ck)][:, :], wqk[:, h, :], a[:, h, ck * IB:(ck + 1) * IB], start=h == 0,
                              stop=h == CH - 1)
                last.then_inc(qk_rdy, 1)

            def values(b, v):
                for jj in range(VB):
                    jt = v * VB + jj
                    for h in range(CH):
                        last = mm(acc[bank_of("values", v)][:, jj * C:(jj + 1) * C], a[:, h, jt * P:(jt + 1) * P], wvt[:, h, :],
                                  start=h == 0, stop=h == CH - 1)
                last.then_inc(v_rdy, 1)

            def bank_read(b, kind, i):
                p = RING.index((kind, i))
                if p < 4:
                    at_least(pe, acc_out, b * (NB * (IT - 1)))
                    at_least(pe, acc_out_v, b * NB)
                    return
                kind, i = RING[p - 4]
                done, per_batch = {"conv1": (c1_done, 2 * NB), "qk": (qk_done, NB), "values": (v_done, VU)}[kind]
                pe.wait_ge(done, b * per_batch + (i + 1))

            def enter(b):
                for kind, i in SEQUENCE:
                    if kind == "max":
                        if i % IT == 0:
                            pe.wait_ge(qk_done, b * NB + (i // IT + 1))
                        max_unit(b * NB, i, (emx, *et)[i % 3], 3)
                        continue
                    bank_read(b, kind, i)
                    if kind == "conv1":
                        conv1(b, i // 2, i % 2)
                    elif kind == "qk":
                        qk(b, i)
                    else:
                        values(b, i)
                at_least(pe, ot_done, b * (2 * NB))
                shift_transposes(b * NB)
                pe.wait_ge(vmax_1, b + 1)
                nc.tensor.transpose(emx[0:1, 0:P], vm1[:, :], ident[:, :]).then_inc(vmax_row, 1)
                pe.wait_ge(m_rdy, b * NB + 1)
                energies(b * (NB * JT), 0, 0)
                energies(b * (NB * JT) + 1, 1, 0)
                pe.wait_ge(vmax_one, b + 1)
                mm(emx[:, P:P + 1], ones[0:1, :], vma[0:1, 0:1], start=True, stop=True).then_inc(vmax_all, 1)

            def blk(b, n, c):
                g = held(pe, b * NB + n)
                s0 = held(pe, g * JT)
                more = c < NB - 1
                for t in range(JT):
                    pe.wait_ge(pl_rdy, s0 + (t + 1))
                    if t + 2 < JT:
                        energies(s0 + (t + 2), t + 2, n)
                    elif more:
                        if t + 2 == JT:
                            pe.wait_ge(m_rdy, g + 2)
                        energies(s0 + (t + 2), t + 2 - JT, n + 1)
                    if c == 0 and t % (JT // VS) == 0:
                        pe.wait_ge(vl_rdy, b * VS + (t // (JT // VS) + 1))
                    units = list(EMAX_AT[t]) if more else []
                    for it in range(IT):
                        if t == 0:
                            if c == 0:
                                pe.wait_ge(v_done, b * VU + VU)
                            elif it < IT - 1:
                                pe.wait_ge(acc_out, g * (IT - 1) + (it - 2))
                            else:
                                pe.wait_ge(acc_out_v, g)
                        pt = slice(it * P, (it + 1) * P)
                        mm(acc[it][:, 0:C + 1], ph[:, t % 4, pt], vh[:, t, 0:C + 1], start=t == 0, stop=False)
                        mm(acc[it][:, 0:C], ph[:, t % 4, pt], vl[:, t, :], start=False, stop=False)
                        last = mm(acc[it][:, 0:C + 1], pl[:, t % 4, pt], vh[:, t, 0:C + 1], start=False, stop=t == JT - 1)
                        if it == IT - 1:
                            last.then_inc(pv_done, 1)
                        elif t == JT - 1:
                            last.then_inc(acc_rdy, 1)
                        if it in (1, 3) and units:
                            max_unit(g + 1, units.pop(0), emx, 1)
                    if c > 0 and t in T_OT:
                        out_transposes(g, T_OT.index(t))
                    if t in T_CV and not (isinstance(g, int) and g == 0):
                        conv2(g - 1, T_CV.index(t))
                    if more and t == T_MT:
                        at_least(pe, y_rdy, g * 2)
                        shift_transposes(g + 1)

            def leave(b):
                for half in range(2):
                    out_transposes(b * NB + NB, half)

            def batch(b):
                enter(b)
                blk(b, 0, 0)
                with pe.Fori(1, NB - 1) as n:
                    blk(b, n, 1)
                blk(b, NB - 1, NB - 1)
                leave(b)

            batch(0)
            with pe.Fori(1, B) as b:
                batch(b)
            for half in range(2):
                conv2(NB * B - 1, half)


N_PAR = 14
PAR_OPS = 3


def _sequence():
    seq = []
    for ck in range(NB + 2):
        if ck < NB:
            seq += [("conv1", 2 * ck), ("conv1", 2 * ck + 1)]
        if 1 <= ck <= NB:
            seq.append(("qk", ck - 1))
        if ck >= 2:
            v, u = 2 * (ck - 2), IT * (ck - 2)
            if ck <= NB:
                seq += [("values", v), ("max", u), ("max", u + 1), ("values", v + 1), ("max", u + 2), ("max", u + 3)]
            else:
                seq += [("max", u + i) for i in range(IT)] + [("values", v), ("values", v + 1)]
    return seq


SEQUENCE = _sequence()
SHIFT_AFTER = ("max", EU - 1)
RING = [x for x in SEQUENCE if x[0] != "max"]


def bank_of(kind, i):
    return RING.index((kind, i)) % 4


EMAX_AT = []
_u = 0
for _t in range(JT):
    _k = min(2 if _t % 5 == 3 else 1, EU - _u)
    EMAX_AT.append(range(_u, _u + _k))
    _u += _k
assert _u == EU
T_SHIFT = 27
T_MT = 27
T_OT = (1, 5)
T_CV = (20, 22)
T_ADD = ((3, 4, 6, 8), (9, 11, 12, 14), (16, 17, 19, 21), (28, 29, 30, 31))
T_RELU = (9, 15, 23, 1)


_INS = ['x', 'L0_conv_conv1_w', 'L0_conv_bn1_s', 'L0_conv_bn1_b', 'L0_conv_q_w', 'L0_conv_q_b', 'L0_conv_k_w',
        'L0_conv_k_b', 'L0_conv_v_w', 'L0_conv_v_b', 'L0_conv_att_gamma', 'L0_conv_bn2_s', 'L0_conv_bn2_b',
        'L0_conv_conv2_w', 'L0_conv_bn3_s', 'L0_conv_bn3_b']


def kernel(**inputs):
    import numpy as np
    import concourse.bacc as bacc
    from concourse.bass_utils import run_bass_kernel_spmd

    nc = bacc.Bacc("TRN2", target_bir_lowering=False, num_devices=1)
    arrays, args = {}, []

    def put(name, a):
        arrays[name] = a
        args.append(nc.dram_tensor(name, a.shape, mybir.dt.from_np(a.dtype), kind="ExternalInput").ap())

    for name in _INS:
        a = np.ascontiguousarray(inputs[name])
        put(f"in_{name}", a.reshape(1) if a.ndim == 0 else a)
    k = np.arange(S)
    put("identity", np.eye(P, dtype=np.float32))
    put("down_weights", (k / (S - 1)).astype(np.float32))
    put("up_weights", np.stack([-k / (H - 1), (S - 1 - k) / (H - 1)], axis=1).astype(np.float32))
    out = nc.dram_tensor("out", (B, C, H, H), F32, kind="ExternalOutput").ap()
    attention_block_kernel(nc, *args, out)
    r = run_bass_kernel_spmd(nc, [arrays], core_ids=[0])
    return r.results[0]["out"]
```

```python
import concourse.bass as bass
from concourse import mybir
from contextlib import ExitStack

F32 = mybir.dt.float32
F32R = mybir.dt.float32r
F16 = mybir.dt.float16
ACT = mybir.ActivationFunctionType
ALU = mybir.AluOpType
AX = mybir.AxisListType

B, C, H, D = 4, 256, 128, 32
S = H // 2
N = S * S
P = 128
CH = C // P
IB = 512
NB = N // IB
IT = IB // P
JT = N // P
JC = N // IB
EU = IT * JC
BR = IB // S
UR = 8
DR = 8
PIECES = 4
VB = 2
VU = JT // VB
LOG_P = 8.0
V_TOP = 2.0 ** 14
BN = 1.0 / (1.0 + 1e-5) ** 0.5
DN, UP = 6, 5
V_OF = (3, 2, 3, 2, 2, 2, 2, 2)


def attention_block_kernel(nc, x, w1, s1, b1, wq, bq, wk, bk, wv, bv, gamma, s2, b2, w2, s3, b3,
                           ident_d, down_w, up_w, out):
    with ExitStack() as ctx:
        def sb(name, shape, dt=F32):
            return ctx.enter_context(nc.sbuf_tensor(name, shape, dt))

        def bank(name):
            return ctx.enter_context(nc.psum_tensor(name, [P, 512], F32))

        def sem(name):
            return ctx.enter_context(nc.semaphore(name))

        xr = sb("xr", [P, NB, CH, BR, S])
        a = sb("a", [P, CH, N])
        ks = sb("ks", [P, N], F32R)
        qs = sb("qs", [P, N], F32R)
        qm = sb("qm", [3 * D, IB], F32R)
        vh = sb("vh", [P, JT, C + 2], F16)
        vl = sb("vl", [P, JT, C], F16)
        ph = sb("ph", [P, 4, IB], F16)
        pl = sb("pl", [P, 4, IB], F16)
        pf = sb("pf", [P, 2, IB])
        osb = sb("osb", [P, IT, C])
        hbuf = sb("hbuf", [P, CH, IB])
        win = sb("win", [P, 2, CH, BR + 2, S])
        xres = sb("xres", [P, 4, UR, H])
        xin = sb("xin", [P, 2, DR, H])
        rd = sb("rd", [P, UR // 2 + 1, S])
        rt = sb("rt", [P, UR // 2, 2, S])
        y2 = sb("y2", [P, UR, S])
        cd = sb("cd", [P, UR, S + 1])
        ct = sb("ct", [P, UR, S, 2])
        dd = sb("dd", [P, DR // 2, S])
        w1t = sb("w1t", [P, CH, C])
        wvt = sb("wvt", [P, CH, C])
        w2t = sb("w2t", [P, CH, C])
        wva = sb("wva", [P, CH, C])
        wqk = sb("wqk", [P, CH, 4 * D])
        ident = sb("ident", [P, P])
        dw = sb("dw", [P, S])
        uw = sb("uw", [P, S, 2])
        par = sb("par", [P, 8, CH])
        S1, B1, S2, B2, S3, B3, BV = range(7)
        gam = sb("gam", [P, 1])
        qkb = sb("qkb", [P, 1])
        mx = sb("mx", [P, IT, JC])
        m4 = sb("m4", [P, IT])
        mn = sb("mn", [P, IT])
        mhl = sb("mhl", [P, IT, 2], F32R)
        am = sb("am", [P, NB, CH])
        am1 = sb("am1", [P, CH])
        vb = sb("vb", [1, 1])
        ones = sb("ones", [1, P])
        vg = sb("vg", [P, 4])
        rl = sb("rl", [P, IT])

        acc = [bank(f"acc{i}") for i in range(IT)]
        et = [bank(f"et{i}") for i in range(2)]
        emx = bank("emx")
        wrk = bank("wrk")

        dw_ld, par_ld, wts_ld = sem("dw_ld"), sem("par_ld"), sem("wts_ld")
        par_ok, wt_rdy, wt_ok, mem_ok, memv_ok = (sem(n) for n in ("par_ok", "wt_rdy", "wt_ok", "mem_ok", "memv_ok"))
        xin_ld = [sem(f"xin_ld{i}") for i in range(2)]
        xres_ld = [sem(f"xres_ld{i}") for i in range(4)]
        stored = [sem(f"stored{i}") for i in range(4)]
        down_p, down_v = sem("down_p"), sem("down_v")
        up_p, up_v = sem("up_p"), sem("up_v")
        up_added, up_relu = sem("up_added"), sem("up_relu")
        c1_rdy, c1_done = sem("c1_rdy"), sem("c1_done")
        qk_rdy, qk_hi, qk_done = sem("qk_rdy"), sem("qk_hi"), sem("qk_done")
        v_rdy, vh_rdy, v_done, vscale = sem("v_rdy"), sem("vh_rdy"), sem("v_done"), sem("vscale")
        amax_part, amax_rdy, bound_row, bound_one, bound_all = (
            sem(n) for n in ("amax_part", "amax_rdy", "bound_row", "bound_one", "bound_all"))
        qm_rdy, emx_rdy, emx_free, m_link, mt_rdy, m_rdy = (
            sem(n) for n in ("qm_rdy", "emx_rdy", "emx_free", "m_link", "mt_rdy", "m_rdy"))
        et_rdy, p_rdy, pl_rdy, pv_done = sem("et_rdy"), sem("p_rdy"), sem("pl_rdy"), sem("pv_done")
        acc_rdy, rl_rdy, acc_out, acc_out_v = sem("acc_rdy"), sem("rl_rdy"), sem("acc_out"), sem("acc_out_v")
        ot_rdy, ot_done, h_rdy = sem("ot_rdy"), sem("ot_done"), sem("h_rdy")
        cv_rdy, y_rdy = sem("cv_rdy"), sem("y_rdy")
        late_v = sem("late_v")

        def at_least(eng, s, value):
            if isinstance(value, int) and value <= 0:
                return
            eng.wait_ge(s, value)

        def walk(eng, enter, block, leave, last_apart=False):
            def batch(b):
                enter(b)
                for n in range(3):
                    block(b, n, n)
                with eng.Fori(0, (NB - 4) // 2) as i:
                    block(b, i * 2 + 3, 3)
                    block(b, i * 2 + 4, 4)
                block(b, NB - 1, NB - 1)
                leave(b)

            batch(0)
            if last_apart:
                with eng.Fori(1, B - 1) as b:
                    batch(b)
                batch(B - 1)
            else:
                with eng.Fori(1, B) as b:
                    batch(b)

        def held(eng, value):
            return value if isinstance(value, int) else eng.snap(value)

        def is_first(b):
            return isinstance(b, int) and b == 0

        def is_last(b, c):
            return isinstance(b, int) and b == B - 1 and c == NB - 1

        def up_pieces(b, n, c):
            for j in range(PIECES):
                back = 3 if j < 3 else 2
                g = b * NB + n
                if isinstance(g, int) and g < back:
                    continue
                wrap = c < back
                yield (j, g * PIECES - 11 + j, b - 1 if wrap else b, n + NB - back if wrap else n - back,
                       (c - back) % 2, (1 + j) % PIECES)
            if is_last(b, c):
                for j in range(PIECES, PIECES + MORE_LAST):
                    yield j, (NB * B - 1) * PIECES - 11 + j, b, n - 2, (n - 2) % 2, (1 + j) % PIECES

        def late_piece(u):
            chunk = u // PIECES
            return (u + 3) % 4, B - 1, chunk - (B - 1) * NB, chunk % 2, u % PIECES

        def xslot(j):
            return (j + 1) % 4

        def piece_rows(n, k):
            return k % 2, (n * (2 * BR) + (k // 2) * UR)

        def dram_rows(t, b, half, row, rows):
            v = t[bass.ds(b, 1), half * P:(half + 1) * P, bass.ds(row, rows), :]
            return v.rearrange("o p r c -> (o p) r c")

        def v_before(ck):
            return sum(V_OF[:ck])

        def p_before(ck):
            return PIECES * ck - v_before(ck)

        V_ALL, P_ALL = v_before(NB), p_before(NB)
        XRES_FIRST = [(V_ALL - s + 3) // 4 for s in range(4)]
        assert P_ALL % 2 == 0

        def down_count(b, d):
            return (b - 1) * (DN * NB * PIECES) + DN * (P_ALL + d)

        nc.disable_value_cache = True
        block = ctx.enter_context(nc.Block())

        @block.sync
        def _(sp):
            sp.dma_start(dw[:], down_w.partition_broadcast(P)).then_inc(dw_ld, 16)

            def load_weights():
                sp.dma_start(ident[:], ident_d).then_inc(wts_ld, 16)
                for dst, t in ((osb[:, 0:2, :], w1), (osb[:, 2:4, :], wv), (hbuf[:, :, 0:C], w2)):
                    sp.dma_start(dst, t.rearrange("(o p) c -> p o c", p=P)).then_inc(wts_ld, 16)
                sp.dma_start(hbuf[0:D, 0, C:2 * C], wk).then_inc(wts_ld, 16)
                sp.dma_start(hbuf[0:D, 1, C:2 * C], wq).then_inc(wts_ld, 16)

            def load_parameters():
                n = 0
                for i, t in ((S1, s1), (B1, b1), (S2, s2), (B2, b2), (S3, s3), (B3, b3), (BV, bv)):
                    sp.dma_start(par[:, i, :], t.rearrange("(h p) -> p h", p=P), allow_slow_non_contiguous=True).then_inc(par_ld, 16)
                    n += 1
                for i, t in enumerate((bk, bk, bq, bq)):
                    sp.dma_start(qkb[i * D:(i + 1) * D, :], t.unsqueeze(1)).then_inc(par_ld, 16)
                    n += 1
                sp.dma_start(gam[:], gamma.partition_broadcast(P)).then_inc(par_ld, 16)
                sp.dma_start(uw[:], up_w.partition_broadcast(P)).then_inc(par_ld, 16)
                assert n + 2 == N_PAR

            for d in (*FIRST_LOADS, *(d for d in range(NB * PIECES) if d not in FIRST_LOADS)):
                ck, j = divmod(d, PIECES)
                if d == FIRST_LOADS[-1]:
                    load_weights()
                    load_parameters()
                src = dram_rows(x, 0, j % 2, (2 * ck + j // 2) * DR, DR)
                if j < V_OF[ck]:
                    i = v_before(ck) + j
                    at_least(sp, down_v, DN * (i - 3))
                    sp.dma_start(xres[:, i % 4], src).then_inc(xres_ld[i % 4], 16)
                else:
                    i = p_before(ck) + j - V_OF[ck]
                    at_least(sp, down_p, DN * (i - 1))
                    sp.dma_start(xin[:, i % 2], src).then_inc(xin_ld[i % 2], 16)

            def load_shortcut(j, u, b, n, k):
                half, row = piece_rows(n, k)
                s = xslot(j)
                uses = (u - s) // 4 if isinstance(u, int) else None
                at_least(sp, stored[s], (u - s) * 4 if uses is None else uses * 16)
                if isinstance(u, int) and u < 4:
                    sp.wait_ge(down_v, DN * V_ALL)
                sp.dma_start(xres[:, s], dram_rows(x, b, half, row, UR)).then_inc(xres_ld[s], 16)

            def enter(b):
                pass

            def blk(b, n, c):
                ups = {j: (u, ub, un, k) for j, u, ub, un, _, k in up_pieces(b, n, c)}
                for j in range(PIECES):
                    if not (isinstance(b, int) and b == B - 1):
                        i = n * PIECES + j
                        sp.wait_ge(down_p, down_count(b + 1, i - 1))
                        sp.dma_start(xin[:, j % 2], dram_rows(x, b + 1, j % 2, (n * 2 + j // 2) * DR, DR)).then_inc(
                            xin_ld[j % 2], 16)
                    if j in ups:
                        load_shortcut(j, *ups[j])
                for j in range(PIECES, len(ups)):
                    load_shortcut(j, *ups[j])

            def leave(b):
                pass

            walk(sp, enter, blk, leave, last_apart=True)
            for u in range(LATE, PIECES * NB * B):
                j, ub, un, _, k = late_piece(u)
                load_shortcut(j, u, ub, un, k)
            for s in range(4):
                sp.wait_ge(stored[s], 16 * B * NB)

        def down_piece(eng, ops, s, count, src, tmp, dst, first_small_row):
            pair = src.rearrange("p (r two) c -> p r two c", two=2)
            even, odd = pair[:, :, 0, :], pair[:, :, 1, :]
            rw = dw[:, bass.ds(first_small_row, DR // 2)].unsqueeze(2).broadcast_to([P, DR // 2, H])
            cw = dw[:, :].unsqueeze(1).broadcast_to([P, DR // 2, S])
            cols = even.rearrange("p r (c two) -> p r c two", two=2)
            ops.tensor_tensor(odd, odd, even, ALU.subtract).then_inc(s, 1)
            eng.wait_ge(s, count + 1)
            ops.tensor_tensor(odd, odd, rw, ALU.mult).then_inc(s, 1)
            eng.wait_ge(s, count + 2)
            ops.tensor_tensor(even, even, odd, ALU.add).then_inc(s, 1)
            eng.wait_ge(s, count + 3)
            ops.tensor_tensor(tmp, cols[:, :, :, 1], cols[:, :, :, 0], ALU.subtract).then_inc(s, 1)
            eng.wait_ge(s, count + 4)
            ops.tensor_tensor(tmp, tmp, cw, ALU.mult).then_inc(s, 1)
            eng.wait_ge(s, count + 5)
            ops.tensor_tensor(dst, cols[:, :, :, 0], tmp, ALU.add).then_inc(s, 1)

        def up_chain(eng, ops, s, base, n, par_, k, buffers, added):
            rd_, rt_, y2_, cd_, ct_ = buffers
            half, q = k % 2, k // 2
            w = win[:, par_, half, q * (BR // 2):q * (BR // 2) + BR // 2 + 2, :]
            R = UR // 2
            ops.tensor_tensor(rd_, w[:, 1:R + 2, :], w[:, 0:R + 1, :], ALU.subtract).then_inc(s, 1)
            eng.wait_ge(s, base + 1)
            first = n * BR + q * R
            for parity in range(2):
                wt = uw[:, bass.ds(first, R), parity:parity + 1].broadcast_to([P, R, S])
                last = ops.tensor_tensor(rt_[:, :, parity, :], rd_[:, parity:parity + R, :], wt, ALU.mult)
            last.then_inc(s, 1)
            eng.wait_ge(s, base + 2)
            at_least(eng, up_v, added * 2)
            mid = w[:, 1:R + 1, :].unsqueeze(2).broadcast_to([P, R, 2, S])
            ops.tensor_tensor(y2_.rearrange("p (r two) c -> p r two c", two=2), mid, rt_, ALU.add).then_inc(s, 1)
            eng.wait_ge(s, base + 3)
            ops.tensor_tensor(cd_[:, :, 1:S], y2_[:, :, 1:S], y2_[:, :, 0:S - 1], ALU.subtract).then_inc(s, 1)
            eng.wait_ge(s, base + 4)
            at_least(eng, up_added, added * 2)
            for parity in range(2):
                wt = uw[:, :, parity].unsqueeze(1).broadcast_to([P, UR, S])
                last = ops.tensor_tensor(ct_[:, :, :, parity], cd_[:, :, parity:parity + S], wt, ALU.mult)
            last.then_inc(s, 1)

        @block.gpsimd
        def _(pool):
            ops = nc.gpsimd
            ops.memset(ks[3 * D:P, :].bitcast(F32), 1.0).then_inc(mem_ok, 1)
            pool.wait_ge(mem_ok, 1)
            ops.memset(vh[:, :, C:C + 2], 1.0).then_inc(mem_ok, 1)
            pool.wait_ge(mem_ok, 2)
            ops.memset(ones[:], 1.0).then_inc(mem_ok, 1)
            pool.wait_ge(mem_ok, 3)
            ops.memset(cd[:], 0.0).then_inc(mem_ok, 1)
            pool.wait_ge(mem_ok, 4)
            pool.wait_ge(dw_ld, 16)
            for i, (ck, j) in enumerate((ck, j) for ck in range(NB) for j in range(V_OF[ck], PIECES)):
                pool.wait_ge(xin_ld[i % 2], 16 * (i // 2 + 1))
                small = (2 * ck + j // 2) * (DR // 2)
                down_piece(pool, ops, down_p, DN * i, xin[:, i % 2], dd[:],
                           xr[:, ck, j % 2, (j // 2) * (DR // 2):(j // 2 + 1) * (DR // 2), :], small)

            pool.wait_ge(par_ld, 16 * N_PAR)

            def up_piece(u, n, par_, k, base, added):
                up_chain(pool, ops, up_p, base, n, par_, k, (rd[:], rt[:], y2[:], cd[:], ct[:]), added)

            def enter(b):
                if not (isinstance(b, int) and b == B - 1):
                    pool.wait_ge(c1_rdy, b * (2 * NB) + 2 * NB)

            def blk(b, n, c):
                ups = {j: (u, un, pr, k) for j, u, _, un, pr, k in up_pieces(b, n, c)}
                g = b * NB + n
                for j in range(max(PIECES, len(ups))):
                    if j in ups:
                        if j == 3:
                            pool.wait_ge(y_rdy, g * 2)
                        u = ups[j][0]
                        up_piece(*ups[j], u * UP, u)
                    if not (isinstance(b, int) and b == B - 1):
                        i = n * PIECES + j
                        fills = P_ALL // 2
                        pool.wait_ge(xin_ld[j % 2], b * (16 * NB * PIECES // 2) + n * 32 + (16 * (fills + j // 2 + 1)))
                        small = (n * 2 + j // 2) * (DR // 2)
                        dst = xr[:, bass.ds(n, 1), j % 2, (j // 2) * (DR // 2):(j // 2 + 1) * (DR // 2), :]
                        down_piece(pool, ops, down_p, down_count(b + 1, i), xin[:, j % 2], dd[:],
                                   dst.rearrange("p o r c -> p (o r) c"), small)

            def leave(b):
                pass

            walk(pool, enter, blk, leave, last_apart=True)
            before = LATE
            for i, u in enumerate(LATE_POOL):
                _, _, un, pr, k = late_piece(u)
                if u == LATE_POOL_LAST_CHUNK:
                    pool.wait_ge(y_rdy, 2 * NB * B)
                up_piece(u, un, pr, k, (LATE + i) * UP, before)
                before = LATE + LATE_ORDER.index(u) + 1

        @block.scalar
        def _(act):
            ops = nc.scalar

            def weights_of(s, t):
                act.wait_ge(et_rdy, s + 1)
                at_least(act, pv_done, s - 3)
                ops.activation(ph[:, t % 4, :], et[t % 2][:, :], ACT.Exp)
                at_least(act, pl_rdy, s - 1)
                ops.activation(pf[:, t % 2, :], et[t % 2][:, :], ACT.Exp).then_inc(p_rdy, 1)

            def relu_h(chunk, half):
                act.wait_ge(ot_done, chunk * 2 + (half + 1))
                ops.activation(hbuf[:, half, :], hbuf[:, half, :], ACT.Relu, bias=par[:, B2, half:half + 1],
                               scale=par[:, S2, half:half + 1]).then_inc(h_rdy, 1)

            def bn3(chunk, par_, half, first, last):
                act.wait_ge(cv_rdy, chunk * 2 + (half + 1))
                if half == 0:
                    at_least(act, up_p, (chunk - 1) * (UP * PIECES))
                    at_least(act, y_rdy, chunk * 2)
                new, old = win[:, par_, half], win[:, 1 - par_, half]
                cv = wrk[:, :].rearrange("p (r c) -> p r c", c=S)
                jobs = [(new[:, 0:1, :], cv[:, 0:1, :])] if first else [(old[:, BR + 1:BR + 2, :], cv[:, 0:1, :])]
                if last:
                    jobs.append((new[:, BR + 1:BR + 2, :], cv[:, BR - 1:BR, :]))
                if not first:
                    ops.copy(new[:, 0, :], old[:, BR, :])
                for dst, src in jobs + [(new[:, 1:BR + 1, :], cv)]:
                    done = ops.activation(dst, src, ACT.Identity, bias=par[:, B3, half:half + 1], scale=par[:, S3, half:half + 1])
                done.then_inc(y_rdy, 1)

            def final_relu(j, i):
                act.wait_ge(up_added, i * 2 + 2)
                ops.activation(xres[:, xslot(j)], xres[:, xslot(j)], ACT.Relu).then_inc(up_relu, 1)

            def store(j, i, b, n, k):
                half, row = piece_rows(n, k)
                act.wait_ge(up_relu, i + 1)
                act.dma_start(dram_rows(out, b, half, row, UR), xres[:, xslot(j)]).then_inc(stored[xslot(j)], 16)

            act.wait_ge(par_ok, PAR_OPS)

            def conv1_out(b, ck, oh):
                u = 2 * ck + oh
                act.wait_ge(c1_rdy, b * (2 * NB) + (u + 1))
                ops.activation(a[:, oh, ck * IB:(ck + 1) * IB], acc[bank_of("conv1", u)][:, :], ACT.Relu,
                               bias=par[:, B1, oh:oh + 1], scale=par[:, S1, oh:oh + 1]).then_inc(c1_done, 1)

            def qk_high(b, ck):
                cs = slice(ck * IB, (ck + 1) * IB)
                act.wait_ge(qk_rdy, b * NB + (ck + 1))
                ps = acc[bank_of("qk", ck)]
                ops.activation(ks[0:2 * D, cs], ps[0:2 * D, :], ACT.Identity, bias=qkb[0:2 * D, :])
                ops.activation(qs[0:2 * D, cs], ps[2 * D:4 * D, :], ACT.Identity, bias=qkb[2 * D:4 * D, :])
                ops.activation(qs[2 * D:3 * D, cs], ps[2 * D:3 * D, :], ACT.Identity,
                               bias=qkb[2 * D:3 * D, :]).then_inc(qk_hi, 1)

            def values_high(b, v):
                if v == 0:
                    act.wait_ge(vscale, b * 4 + 4)
                act.wait_ge(v_rdy, b * VU + (v + 1))
                ops.activation(vh[:, v * VB:(v + 1) * VB, 0:C], acc[bank_of("values", v)][:, :].rearrange("p (j c) -> p j c", c=C),
                               ACT.Copy, scale=vg[:, 2:3]).then_inc(vh_rdy, 1)

            def enter(b):
                for kind, i in A_SEQUENCE:
                    if kind == "conv1":
                        conv1_out(b, i // 2, i % 2)
                        if i == 1 and not is_first(b):
                            for half in range(2):
                                relu_h(b * NB - 1, half)
                    elif kind == "qk":
                        qk_high(b, i)
                    elif kind == "values":
                        values_high(b, i)
                    elif kind == "energies":
                        weights_of(b * (NB * JT) + i, i)

            def blk(b, n, c):
                g = held(act, b * NB + n)
                s0 = held(act, g * JT)
                ups = {j: (u, ub, un, k) for j, u, ub, un, _, k in up_pieces(b, n, c)}
                before = {}
                if not (isinstance(g, int) and g < 3):
                    before = {j: (u, ub, un, k) for j, u, ub, un, _, k in
                              (up_pieces(b, n - 1, c - 1) if c else up_pieces(b - 1, NB - 1, NB - 1))}
                t_cv, t_relu = (T_CV_LAST, T_RELU_LAST) if is_last(b, c) else (T_CV, T_RELU if c < NB - 1 else T_RELU_7)
                for t in range(JT):
                    if c > 0 and t in (T_OT[0] + 2, T_OT[1] + 2):
                        relu_h(g - 1, T_OT.index(t - 2))
                    if t in (t_cv[0] + 1, t_cv[1] + 1) and not (isinstance(g, int) and g == 0):
                        bn3(g - 1, (c - 1) % 2, t_cv.index(t - 1), c == 1, c == 0)
                    if t in t_relu and t_relu.index(t) in ups:
                        final_relu(t_relu.index(t), ups[t_relu.index(t)][0])
                    if t - 1 in t_relu and t_relu.index(t - 1) in ups:
                        store(t_relu.index(t - 1), *ups[t_relu.index(t - 1)])
                    if t == T_RELU_BEFORE and 3 in before:
                        final_relu(3, before[3][0])
                    if t == T_RELU_BEFORE + 1 and 3 in before:
                        store(3, *before[3])
                    if t == JT - 1:
                        for it in range(IT - 1):
                            act.wait_ge(rl_rdy, g * IT + (it + 1))
                            ops.activation(osb[:, it, :], acc[it][:, 0:C], ACT.Copy, scale=rl[:, it:it + 1]).then_inc(acc_out, 1)
                    if t + AHEAD < JT or c < NB - 1:
                        weights_of(s0 + (t + AHEAD), (t + AHEAD) % JT)

            def leave(b):
                pass

            walk(act, enter, blk, leave, last_apart=True)
            for half in range(2):
                relu_h(NB * B - 1, half)
            ups = list(up_pieces(B - 1, NB - 1, NB - 1))
            for j, u, ub, un, _, k in ups[len(T_RELU_LAST):]:
                final_relu(j, u)
                store(j, u, ub, un, k)
            for half in range(2):
                bn3(NB * B - 1, (NB - 1) % 2, half, False, True)
            for i, u in enumerate(LATE_ORDER):
                j, ub, un, _, k = late_piece(u)
                final_relu(j, LATE + i)
                store(j, LATE + i, ub, un, k)

        @block.vector
        def _(dve):
            ops = nc.vector
            ops.memset(qs[3 * D:P, :].bitcast(F32), 0.0).then_inc(memv_ok, 1)
            def transposed_weights():
                for i, dst in enumerate((w1t, wvt, w2t)):
                    dve.wait_ge(wt_rdy, i + 1)
                    ops.tensor_copy(dst[:].rearrange("p h c -> p (h c)"), acc[i][:, :])
                dve.wait_ge(wt_rdy, 4)
                for i in range(4):
                    last = ops.tensor_copy(wqk[:, :, i * D:(i + 1) * D],
                                           acc[3][:, 0:4 * D].rearrange("p (w h d) -> p w h d", w=2, h=CH)[:, i // 2])
                last.then_inc(wt_ok, 1)
                dve.wait_ge(wt_ok, 1)
                ops.scalar_tensor_tensor(wva[:], wvt[:], -1.0, wvt[:], ALU.mult, ALU.max).then_inc(wt_ok, 1)

            def first_down(ck):
                for j in range(V_OF[ck]):
                    i = v_before(ck) + j
                    dve.wait_ge(xres_ld[i % 4], 16 * (i // 4 + 1))
                    small = (2 * ck + j // 2) * (DR // 2)
                    down_piece(dve, ops, down_v, DN * i, xres[:, i % 4], rt[:, :, 0, :],
                               xr[:, ck, j % 2, (j // 2) * (DR // 2):(j // 2 + 1) * (DR // 2), :], small)

            dve.wait_ge(dw_ld, 16)
            first_down(0)
            transposed_weights()
            dve.wait_ge(par_ld, 16 * N_PAR)
            for i in (S1, S2, S3):
                ops.tensor_scalar(par[:, i, :], par[:, i, :], BN, None, ALU.mult)
            ops.tensor_scalar(par[:, BV, :], par[:, BV, :], gam[:, 0:1], None, ALU.mult).then_inc(par_ok, 1)
            dve.wait_ge(par_ok, 1)
            ops.tensor_tensor(par[:, BV, :], par[:, BV, :], par[:, S2, :], ALU.mult).then_inc(par_ok, 1)
            dve.wait_ge(par_ok, 2)
            ops.tensor_tensor(par[:, B2, :], par[:, B2, :], par[:, BV, :], ALU.add).then_inc(par_ok, 1)
            first_down(1)

            def row_max(g, u, bank):
                dve.wait_ge(emx_rdy, g * EU + (u + 1))
                ops.reduce_max(mx[:, u % IT, u // IT:u // IT + 1], bank[:, :], AX.X).then_inc(emx_free, 1)

            def next_max(g, units):
                u = units.pop(0)
                row_max(g, u, (emx, wrk)[MAX_BANK[u]])

            def shift(g):
                dve.wait_ge(emx_free, g * EU + EU)
                ops.reduce_max(m4[:], mx[:], AX.X).then_inc(m_link, 1)
                dve.wait_ge(m_link, g * 4 + 1)
                ops.tensor_scalar(mn[:], m4[:], -1.0, LOG_P, ALU.mult, ALU.add).then_inc(m_link, 1)
                dve.wait_ge(m_link, g * 4 + 2)
                ops.tensor_copy(mhl[:, :, 0], mn[:]).then_inc(m_link, 1)
                dve.wait_ge(m_link, g * 4 + 3)
                ops.tensor_tensor(mhl[:, :, 1], mn[:], mhl[:, :, 0].bitcast(F32), ALU.subtract).then_inc(m_link, 1)

            def shift_rows(g, n):
                dve.wait_ge(mt_rdy, g + 1)
                ops.tensor_copy(qs[3 * D:3 * D + 2, bass.ds(n * IB, IB)], wrk[0:2, :]).then_inc(m_rdy, 1)

            def low_parts(s, t):
                dve.wait_ge(p_rdy, s + 1)
                at_least(dve, pv_done, s - 3)
                ops.tensor_tensor(pl[:, t % 4, :], pf[:, t % 2, :], ph[:, t % 4, :], ALU.subtract).then_inc(pl_rdy, 1)

            def copy_queries(n):
                ops.tensor_copy(qm[:, :], qs[0:3 * D, bass.ds(n * IB, IB)].bitcast(F32)).then_inc(qm_rdy, 1)

            def residual(chunk, n, half):
                dve.wait_ge(ot_rdy, chunk * 2 + (half + 1))
                at_least(dve, cv_rdy, chunk * 2)
                ops.scalar_tensor_tensor(hbuf[:, half, :], wrk[:, :], vg[:, 3:4], a[:, half, bass.ds(n * IB, IB)], ALU.mult,
                                         ALU.add).then_inc(ot_done, 1)

            def add_piece(j, u, part):
                if part == 0:
                    dve.wait_ge(up_p, u * UP + UP)
                add_part(j, u, part, u, y2, ct)

            def add_part(j, u, part, i, y2, ct):
                rs = slice((part % 2) * (UR // 2), (part % 2 + 1) * (UR // 2))
                xs = xres[:, xslot(j), rs, :]
                if part == 0:
                    dve.wait_ge(xres_ld[xslot(j)], (u - xslot(j)) * 4 + 16 * (XRES_FIRST[xslot(j)] + 1))
                if part < 2:
                    xs4 = xs.rearrange("p r (c two) -> p r c two", two=2)
                    ops.tensor_tensor(xs4, xs4, y2[:, rs].unsqueeze(3).broadcast_to([P, UR // 2, S, 2]), ALU.add).then_inc(up_v, 1)
                else:
                    dve.wait_ge(up_v, i * 2 + (part - 1))
                    ops.tensor_tensor(xs, xs, ct[:, rs].rearrange("p r c two -> p r (c two)"), ALU.add).then_inc(up_added, 1)

            def qk_low(b, ck):
                cs = slice(ck * IB, (ck + 1) * IB)
                dve.wait_ge(qk_hi, b * NB + (ck + 1))
                ps = acc[bank_of("qk", ck)]
                ops.tensor_copy(ks[2 * D:3 * D, cs], ks[0:D, cs].bitcast(F32))
                for t, r in ((ks, slice(D, 2 * D)), (qs, slice(2 * D, 3 * D))):
                    last = ops.scalar_tensor_tensor(t[r, cs], ps[r, :], qkb[r, :], t[r, cs].bitcast(F32), ALU.add, ALU.subtract)
                last.then_inc(qk_done, 1)
                if ck == 0:
                    dve.wait_ge(qk_done, b * NB + 1)
                    copy_queries(0)

            def largest_a(b, ck):
                dve.wait_ge(c1_done, b * (2 * NB) + (2 * ck + 2))
                ops.reduce_max(am[:, ck, :], a[:, :, ck * IB:(ck + 1) * IB], AX.X).then_inc(amax_part, 1)

            def values_low(b, v):
                dve.wait_ge(vh_rdy, b * VU + (v + 1))
                js = slice(v * VB, (v + 1) * VB)
                ops.scalar_tensor_tensor(vl[:, js, :], acc[bank_of("values", v)][:, :].rearrange("p (j c) -> p j c", c=C),
                                         vg[:, 2:3], vh[:, js, 0:C], ALU.mult, ALU.subtract).then_inc(v_done, 1)

            def enter(b):
                for kind, i in V_SEQUENCE:
                    if kind == "conv1":
                        if i % 2 == 0 and is_first(b) and i // 2 + 2 < NB:
                            first_down(i // 2 + 2)
                    elif kind == "qk":
                        if i < NB - 1:
                            largest_a(b, i)
                        qk_low(b, i)
                    elif kind == "max":
                        row_max(b * NB, i, (emx, *et)[i % 3])
                        if i == EU - 1:
                            shift(b * NB)
                    elif kind == "bound_row":
                        largest_a(b, NB - 1)
                        dve.wait_ge(amax_part, b * NB + NB)
                        ops.reduce_max(am1[:], am[:].rearrange("p k h -> p h k"), AX.X).then_inc(amax_rdy, 1)
                    elif kind == "bound_all":
                        dve.wait_ge(bound_row, b + 1)
                        ops.reduce_max(vb[:], wrk[0:1, 0:C], AX.X).then_inc(bound_one, 1)
                    elif kind == "scale":
                        dve.wait_ge(bound_all, b + 1)
                        ops.tensor_scalar(vg[:, 0:1], wrk[:, C:C + 1], 1e-30, None, ALU.max).then_inc(vscale, 1)
                        dve.wait_ge(vscale, b * 4 + 1)
                        ops.reciprocal(vg[:, 1:2], vg[:, 0:1]).then_inc(vscale, 1)
                        ops.tensor_scalar(vg[:, 3:4], vg[:, 0:1], gam[:, 0:1], 1.0 / V_TOP, ALU.mult, ALU.mult).then_inc(vscale, 1)
                        dve.wait_ge(vscale, b * 4 + 2)
                        ops.tensor_scalar(vg[:, 2:3], vg[:, 1:2], V_TOP, None, ALU.mult).then_inc(vscale, 1)
                        dve.wait_ge(vscale, b * 4 + 4)
                    elif kind == "values":
                        values_low(b, i)
                    elif kind == "shift_rows":
                        shift_rows(b * NB, 0)
                    elif kind == "energies" and i < 2:
                        low_parts(b * (NB * JT) + i, i)

            def row_sum(g, it):
                if it < IT - 1:
                    dve.wait_ge(acc_rdy, g * (IT - 1) + (it + 1))
                else:
                    dve.wait_ge(pv_done, g * JT + JT)
                ops.reciprocal(rl[:, it:it + 1], acc[it][:, C:C + 1]).then_inc(rl_rdy, 1)

            def blk(b, n, c):
                g = held(dve, b * NB + n)
                s0 = held(dve, g * JT)
                more = c < NB - 1
                ups = {j: u for j, u, _, _, _, _ in up_pieces(b, n, c)}
                if more:
                    copy_queries(n + 1)
                for t in range(JT):
                    if more and t == T_MT + 1:
                        shift_rows(g + 1, n + 1)
                    if more and t == T_SHIFT:
                        shift(g + 1)
                    units = list(EMAX_AT[t]) if more else []
                    if units:
                        next_max(g + 1, units)
                    if t == JT - 1:
                        for it in range(IT):
                            row_sum(g, it)
                        dve.wait_ge(rl_rdy, g * IT + IT)
                        ops.tensor_scalar(osb[:, IT - 1, :], acc[IT - 1][:, 0:C], rl[:, IT - 1:IT], None,
                                          ALU.mult).then_inc(acc_out_v, 1)
                    if t + 2 < JT or more:
                        low_parts(s0 + (t + 2), (t + 2) % JT)
                    if units:
                        next_max(g + 1, units)
                    if c > 0 and t in (T_OT[0] + 1, T_OT[1] + 1):
                        residual(g - 1, n - 1, T_OT.index(t - 1))
                    t_add = T_ADD_LAST if is_last(b, c) else T_ADD if more else T_ADD_7
                    for j in ups:
                        for part in range(4):
                            if t == t_add[j][part]:
                                add_piece(j, ups[j], part)

            def leave(b):
                for half in range(2):
                    residual(b * NB + (NB - 1), NB - 1, half)

            walk(dve, enter, blk, leave, last_apart=True)

            free = xr[:].rearrange("p k h r c -> p (k h r c)")
            sizes = [(UR // 2 + 1) * S, UR * S, UR * S, UR * (S + 1), 2 * UR * S]
            at = [sum(sizes[:i]) for i in range(5)]
            rd_, rt_, y2_, cd_, ct_ = (free[:, o:o + z] for o, z in zip(at, sizes))
            cd_ = cd_.rearrange("p (r c) -> p r c", c=S + 1)
            buffers = (rd_.rearrange("p (r c) -> p r c", c=S), rt_.rearrange("p (r two c) -> p r two c", two=2, c=S),
                       y2_.rearrange("p (r c) -> p r c", c=S), cd_, ct_.rearrange("p (r c two) -> p r c two", two=2, c=S))
            ops.memset(cd_, 0.0).then_inc(late_v, 1)
            done = 1
            for i, u in enumerate(LATE_ORDER):
                j, _, un, pr, k = late_piece(u)
                if u in LATE_POOL:
                    dve.wait_ge(up_p, (LATE + LATE_POOL.index(u) + 1) * UP)
                    y2_c, ct_c = y2, ct
                else:
                    dve.wait_ge(y_rdy, 2 * min(NB * B, u // PIECES + (2 if k > 1 else 1)))
                    dve.wait_ge(late_v, done)
                    up_chain(dve, ops, late_v, done, un, pr, k, buffers, LATE + i)
                    done += UP
                    dve.wait_ge(late_v, done)
                    y2_c, ct_c = buffers[2], buffers[4]
                for part in range(4):
                    add_part(j, u, part, LATE + i, y2_c, ct_c)

        @block.tensor
        def _(pe):
            mm = nc.tensor.matmul
            pe.wait_ge(wts_ld, 16 * 6)
            for i, nat in enumerate((osb[:, 0:2, :], osb[:, 2:4, :], hbuf[:, :, 0:C])):
                for h in range(CH):
                    for o in range(CH):
                        last = nc.tensor.transpose(acc[i][:, (h * CH + o) * P:(h * CH + o + 1) * P],
                                                   nat[:, o, h * P:(h + 1) * P], ident[:, :])
                last.then_inc(wt_rdy, 1)
            for i in range(2):
                for h in range(CH):
                    last = nc.tensor.transpose(acc[3][:, (i * CH + h) * D:(i * CH + h + 1) * D],
                                               hbuf[0:D, i, C + h * P:C + (h + 1) * P], ident[0:D, 0:D])
            last.then_inc(wt_rdy, 1)
            pe.wait_ge(wt_ok, 2)
            pe.wait_ge(mem_ok, 4)
            pe.wait_ge(memv_ok, 1)

            def max_unit(g, u, bank, before):
                jc, it = divmod(u, IT)
                if u == 0:
                    pe.wait_ge(qm_rdy, g + 1)
                at_least(pe, emx_free, g * EU + before)
                mm(bank[:, :], qm[:, it * P:(it + 1) * P], ks[0:3 * D, jc * IB:(jc + 1) * IB], start=True,
                   stop=True).then_inc(emx_rdy, 1)

            def shift_transposes(g):
                pe.wait_ge(m_link, g * 4 + 4)
                for it in range(IT):
                    last = nc.tensor.transpose(wrk[0:2, it * P:(it + 1) * P], mhl[:, it, :].bitcast(F32), ident[:, :])
                last.then_inc(mt_rdy, 1)

            def energies(s, t, n):
                at_least(pe, p_rdy, s - 1)
                mm(et[t % 2][:, :], ks[0:3 * D + 2, t * P:(t + 1) * P], qs[0:3 * D + 2, bass.ds(n * IB, IB)], start=True,
                   stop=True).then_inc(et_rdy, 1)

            def out_transposes(g, half):
                pe.wait_ge(acc_out, g * (IT - 1))
                pe.wait_ge(acc_out_v, g)
                if not half:
                    at_least(pe, y_rdy, g * 2 - 2)
                if half:
                    pe.wait_ge(ot_done, g * 2 - 1)
                for it in range(IT):
                    last = nc.tensor.transpose(wrk[:, it * P:(it + 1) * P], osb[:, it, half * P:(half + 1) * P], ident[:, :])
                last.then_inc(ot_rdy, 1)

            def conv2(chunk, half):
                pe.wait_ge(h_rdy, chunk * 2 + 2)
                if half:
                    pe.wait_ge(y_rdy, chunk * 2 + 1)
                for h in range(CH):
                    last = mm(wrk[:, :], w2t[:, h, half * P:(half + 1) * P], hbuf[:, h, :], start=h == 0, stop=h == CH - 1)
                last.then_inc(cv_rdy, 1)

            def conv1(b, ck, oh):
                if oh == 0:
                    if is_first(b):
                        pe.wait_ge(down_v, DN * v_before(ck + 1))
                        pe.wait_ge(down_p, DN * p_before(ck + 1))
                    else:
                        pe.wait_ge(down_p, down_count(b, PIECES * (ck + 1)))
                for h in range(CH):
                    last = mm(acc[bank_of("conv1", 2 * ck + oh)][:, :], w1t[:, h, oh * P:(oh + 1) * P], xr[:, ck, h].rearrange("p r c -> p (r c)"),
                              start=h == 0, stop=h == CH - 1)
                last.then_inc(c1_rdy, 1)

            def qk(b, ck):
                pe.wait_ge(c1_done, b * (2 * NB) + (2 * ck + 2))
                for h in range(CH):
                    last = mm(acc[bank_of("qk", ck)][:, :], wqk[:, h, :], a[:, h, ck * IB:(ck + 1) * IB], start=h == 0,
                              stop=h == CH - 1)
                last.then_inc(qk_rdy, 1)

            def values(b, v):
                for jj in range(VB):
                    jt = v * VB + jj
                    for h in range(CH):
                        last = mm(acc[bank_of("values", v)][:, jj * C:(jj + 1) * C], a[:, h, jt * P:(jt + 1) * P], wvt[:, h, :],
                                  start=h == 0, stop=h == CH - 1)
                last.then_inc(v_rdy, 1)

            def bank_read(b, kind, i):
                p = RING.index((kind, i))
                if p < IT - 1:
                    at_least(pe, acc_out, 0 if is_first(b) else b * (NB * (IT - 1)) + (p + 2 - IT))
                    return
                if p < IT:
                    at_least(pe, acc_out_v, b * NB)
                    return
                kind, i = RING[p - 4]
                done, per_batch = {"conv1": (c1_done, 2 * NB), "qk": (qk_done, NB), "values": (v_done, VU)}[kind]
                pe.wait_ge(done, b * per_batch + (i + 1))

            def enter(b):
                for kind, i in SEQUENCE:
                    if kind == "max":
                        if i % IT == 0:
                            pe.wait_ge(qk_done, b * NB + (i // IT + 1))
                        max_unit(b * NB, i, (emx, *et)[i % 3], i - 2)
                    elif kind == "bound_row":
                        pe.wait_ge(amax_rdy, b + 1)
                        at_least(pe, ot_done, b * (2 * NB))
                        for h in range(CH):
                            last = mm(wrk[0:1, 0:C], am1[:, h:h + 1], wva[:, h, :], start=h == 0, stop=h == CH - 1)
                        last.then_inc(bound_row, 1)
                    elif kind == "bound_all":
                        pe.wait_ge(bound_one, b + 1)
                        mm(wrk[:, C:C + 1], ones[0:1, :], vb[0:1, 0:1], start=True, stop=True).then_inc(bound_all, 1)
                    elif kind == "shift":
                        pe.wait_ge(vscale, b * 4 + 1)
                        shift_transposes(b * NB)
                    elif kind == "energies":
                        if i == 0:
                            pe.wait_ge(m_rdy, b * NB + 1)
                        energies(b * (NB * JT) + i, i, 0)
                    elif kind in ("conv1", "qk", "values"):
                        bank_read(b, kind, i)
                        if kind == "conv1":
                            conv1(b, i // 2, i % 2)
                            if i < 2 and not is_first(b):
                                out_transposes(b * NB, i)
                        elif kind == "qk":
                            qk(b, i)
                        else:
                            values(b, i)

            def blk(b, n, c):
                g = held(pe, b * NB + n)
                s0 = held(pe, g * JT)
                more = c < NB - 1
                t_cv = T_CV_LAST if is_last(b, c) else T_CV
                for steps in [(t,) for t in range(JT - 2)] + [(JT - 2, JT - 1)]:
                    t, t_end = steps[0], steps[-1]
                    units = list(EMAX_AT[t]) if more else []
                    ahead = [u + AHEAD for u in steps if u + AHEAD < JT or more]
                    for it in range(IT):
                        if t == 0:
                            if c == 0:
                                pe.wait_ge(v_done, b * VU + (VU - IT + 1 + it))
                            elif it < IT - 1:
                                pe.wait_ge(acc_out, g * (IT - 1) + (it - 2))
                            else:
                                pe.wait_ge(acc_out_v, g)
                        pt = slice(it * P, (it + 1) * P)
                        for tt in steps:
                            if it == 0:
                                pe.wait_ge(pl_rdy, s0 + (tt + 1))
                            mm(acc[it][:, 0:C + 1], ph[:, tt % 4, pt], vh[:, tt, 0:C + 1], start=tt == 0, stop=False)
                            mm(acc[it][:, 0:C], ph[:, tt % 4, pt], vl[:, tt, :], start=False, stop=False)
                            last = mm(acc[it][:, 0:C + 1], pl[:, tt % 4, pt], vh[:, tt, 0:C + 1], start=False, stop=tt == JT - 1)
                        if it == IT - 1:
                            last.then_inc(pv_done, len(steps))
                        elif t_end == JT - 1:
                            last.then_inc(acc_rdy, 1)
                        if ahead and (it == 2 or it == 0 and len(ahead) == 2):
                            e = ahead.pop(0)
                            if e == JT:
                                pe.wait_ge(m_rdy, g + 2)
                            energies(s0 + e, e % JT, n + e // JT)
                        if units and it in ((1,) if len(EMAX_AT[t]) == 1 else (0, 3)):
                            u = units.pop(0)
                            if u == FIRST_IN_WRK:
                                at_least(pe, ot_done, g * 2)
                            if u == FIRST_AFTER_CONV2:
                                at_least(pe, y_rdy, g * 2)
                            max_unit(g + 1, u, (emx, wrk)[MAX_BANK[u]], MAX_BEFORE[u])
                    if c > 0 and t in T_OT:
                        out_transposes(g, T_OT.index(t))
                    if t in t_cv and not (isinstance(g, int) and g == 0):
                        if more and t == T_CV[0]:
                            pe.wait_ge(emx_free, (g + 1) * EU + LAST_BEFORE_CONV2 + 1)
                        conv2(g - 1, t_cv.index(t))
                    if more and t == T_MT:
                        shift_transposes(g + 1)

            def batch(b):
                enter(b)
                blk(b, 0, 0)
                with pe.Fori(1, NB - 1) as n:
                    blk(b, n, 1)
                blk(b, NB - 1, NB - 1)

            batch(0)
            with pe.Fori(1, B - 1) as b:
                batch(b)
            batch(B - 1)
            for half in range(2):
                out_transposes(NB * B, half)
            for half in range(2):
                conv2(NB * B - 1, half)


FIRST_LOADS = (0, 3, 1, 2, 6, 4)
N_PAR = 13
PAR_OPS = 3


def _sequence(vector):
    seq = []
    for ck in range(NB):
        m = [("max", u) for u in range(IT * (ck - 2), IT * (ck - 1))] if ck >= 2 else []
        first, second, middle = [("conv1", 2 * ck)], [("conv1", 2 * ck + 1)], [("qk", ck - 1)] if ck else []
        seq += first + second + m[:3] + middle + m[3:] if vector else first + m[:2] + middle + m[2:3] + second + m[3:]
    m = [("max", u) for u in range(EU - 2 * IT, EU)]
    v = [("values", i) for i in range(VU)]
    row, one, scale, qk = ("bound_row", 0), ("bound_all", 0), ("scale", 0), ("qk", NB - 1)
    if vector:
        seq += [row, m[0], m[1], one, scale, m[2], qk, v[0], m[3], m[4], m[5], v[1], m[6], v[2], m[7], *v[3:6]]
    else:
        seq += [v[0], m[0], m[1], row, qk, one, m[2], v[1], m[3], v[2], m[4], m[5], v[3], m[6], v[4], m[7], v[5]]
    beside = {6: "shift", 8: "shift_rows", 10: "energies", 12: "energies", 14: "energies"}
    for i in range(6, VU):
        seq.append(v[i])
        if i in beside:
            seq.append((beside[i], (i - 10) // 2))
    return seq


SEQUENCE, V_SEQUENCE = _sequence(False), _sequence(True)
A_SEQUENCE = [x for x in SEQUENCE if x != ("values", 0)]
A_SEQUENCE.insert(A_SEQUENCE.index(("qk", NB - 1)) + 1, ("values", 0))
RING = [x for x in SEQUENCE if x[0] in ("conv1", "qk", "values")]
assert [RING.index(("values", VU - IT + i)) % IT for i in range(IT)] == list(range(IT))


def bank_of(kind, i):
    return RING.index((kind, i)) % 4


AHEAD = 3
T_OT = (1, 5)
T_CV = (20, 22)
T_WRK = (8, T_CV[0])
EMAX_AT, MAX_BANK, MAX_BEFORE = [], [], []
_last = [None, None]
for _t in range(JT):
    _two = T_WRK[0] <= _t < T_WRK[1]
    _k = 0 if _t == 0 else 2 if _t in (10, 12, 14, 16, 18, 24, 25) else 1
    _k = min(_k, EU - len(MAX_BANK))
    EMAX_AT.append(range(len(MAX_BANK), len(MAX_BANK) + _k))
    for _i in range(_k):
        _b = 1 - MAX_BANK[-1] if _i == 1 or _two else 0
        MAX_BEFORE.append(0 if _last[_b] is None else _last[_b] + 1)
        _last[_b] = len(MAX_BANK)
        MAX_BANK.append(_b)
assert len(MAX_BANK) == EU
_wrk_units = [_u for _u in range(EU) if MAX_BANK[_u]]
FIRST_IN_WRK = _wrk_units[0]
LAST_BEFORE_CONV2 = max(_u for _u in _wrk_units if _u < EMAX_AT[T_CV[0]][0])
FIRST_AFTER_CONV2 = min(_u for _u in _wrk_units if _u > EMAX_AT[T_CV[1]][0])
T_SHIFT = 26
T_MT = 27
T_ADD = ((4, 5, 6, 8), (12, 13, 14, 16), (18, 20, 21, 22), (28, 28, 29, 29))
T_RELU = (9, 17, 24)
T_ADD_7 = ((4, 5, 6, 8), (14, 15, 16, 17), (22, 23, 24, 25), (29, 30, 31, 31))
T_RELU_7 = (9, 19, 27)
T_RELU_BEFORE = 1
MORE_LAST = 2
T_CV_LAST = (12, 14)
T_ADD_LAST = ((1, 3, 4, 5), (7, 8, 9, 10), (11, 12, 13, 14), (20, 21, 22, 23), (25, 26, 27, 28), (30, 30, 31, 31))
T_RELU_LAST = (6, 11, 16, 24, 29)
LATE = PIECES * (NB * B - 1) - 11 + PIECES + MORE_LAST
LATE_ORDER = tuple(LATE + i for i in (0, 2, 1, 4, 3, 6, 5, 8, 7))
LATE_POOL = tuple(LATE + i for i in (0, 1, 3, 5, 7))
LATE_POOL_LAST_CHUNK = PIECES * (NB * B - 1) - 2
assert sorted(LATE_ORDER) == list(range(LATE, PIECES * NB * B)) and LATE_POOL_LAST_CHUNK in LATE_POOL



_INS = ['x', 'L0_conv_conv1_w', 'L0_conv_bn1_s', 'L0_conv_bn1_b', 'L0_conv_q_w', 'L0_conv_q_b', 'L0_conv_k_w',
        'L0_conv_k_b', 'L0_conv_v_w', 'L0_conv_v_b', 'L0_conv_att_gamma', 'L0_conv_bn2_s', 'L0_conv_bn2_b',
        'L0_conv_conv2_w', 'L0_conv_bn3_s', 'L0_conv_bn3_b']


def kernel(**inputs):
    import numpy as np
    import concourse.bacc as bacc
    from concourse.bass_utils import run_bass_kernel_spmd

    nc = bacc.Bacc("TRN2", target_bir_lowering=False, num_devices=1)
    arrays, args = {}, []

    def put(name, a):
        arrays[name] = a
        args.append(nc.dram_tensor(name, a.shape, mybir.dt.from_np(a.dtype), kind="ExternalInput").ap())

    for name in _INS:
        a = np.ascontiguousarray(inputs[name])
        put(f"in_{name}", a.reshape(1) if a.ndim == 0 else a)
    k = np.arange(S)
    put("identity", np.eye(P, dtype=np.float32))
    put("down_weights", (k / (S - 1)).astype(np.float32))
    put("up_weights", np.stack([-k / (H - 1), (S - 1 - k) / (H - 1)], axis=1).astype(np.float32))
    out = nc.dram_tensor("out", (B, C, H, H), F32, kind="ExternalOutput").ap()
    attention_block_kernel(nc, *args, out)
    r = run_bass_kernel_spmd(nc, [arrays], core_ids=[0])
    return r.results[0]["out"]
```
